# Optimizing a Trainium2 kernel written in Bass

```python
import numpy as np
import jax
import jax.numpy as jnp

def _softmax(x, axis=-1):
    return jax.nn.softmax(x, axis=axis)

def _gelu(x):
    return jax.nn.gelu(x, approximate=True)

def _silu(x):
    return jax.nn.silu(x)

def _sigmoid(x):
    return jax.nn.sigmoid(x)

def _layernorm(x, axis=-1, eps=1e-05):
    m = jnp.mean(x, axis=axis, keepdims=True)
    v = jnp.var(x, axis=axis, keepdims=True)
    return (x - m) / jnp.sqrt(v + eps)

def _scatter_add(tgt, idx, src, axis=0):
    return tgt.at[idx].add(src)

def _segment_sum(src, seg, n):
    return jax.ops.segment_sum(src, seg, n)
kernel_name = 'mk_sandwich_d2_jaxref_r8_a08c00'

def setup_inputs(seed: int=0):
    np.random.seed(seed)
    _w = jnp.asarray

    def _L0_attn_setup():
        import jax, jax.numpy as jnp
        import numpy as np
        D_MODEL = 128
        N_HEADS = 16
        D_HEAD = D_MODEL // N_HEADS
        M_SLOPE = 0.5
        BATCH = 2
        SEQ = 256

        def _alibi_bias(n_heads, seq_len, m, dtype):
            slopes = m ** jnp.arange(n_heads, dtype=dtype)
            pos = jnp.arange(seq_len, dtype=dtype)
            dist = jnp.abs(pos[:, None] - pos[None, :])
            return -dist[None, :, :] * slopes[:, None, None]
        key = jax.random.key(seed)
        k1, k2, k3 = jax.random.split(key, 3)
        x = jax.random.normal(k1, (BATCH, SEQ, D_MODEL), dtype=jnp.float32)
        qkv_w = jax.random.normal(k2, (3 * D_MODEL, D_MODEL), dtype=jnp.float32) * (1.0 / np.sqrt(D_MODEL))
        qkv_b = jnp.zeros((3 * D_MODEL,), dtype=jnp.float32)
        out_w = jax.random.normal(k3, (D_MODEL, D_MODEL), dtype=jnp.float32) * (1.0 / np.sqrt(D_MODEL))
        out_b = jnp.zeros((D_MODEL,), dtype=jnp.float32)
        return {'x': x, 'qkv_w': qkv_w, 'qkv_b': qkv_b, 'out_w': out_w, 'out_b': out_b}
    _L0_attn_in = _L0_attn_setup()

    def _L0_ffn_setup():
        import jax, jax.numpy as jnp
        import numpy as np
        B, S, IN, OUT, E, R = (8, 512, 128, 128, 8, 8)
        LORA_ALPHA = 16
        SCALING = LORA_ALPHA / R
        key = jax.random.key(seed)
        k = jax.random.split(key, 6)
        x = jax.random.normal(k[0], (B, S, IN), dtype=jnp.float32)
        base_w = jax.random.normal(k[1], (OUT, IN), dtype=jnp.float32) * 0.02
        base_b = jnp.zeros((OUT,), dtype=jnp.float32)
        lora_A = jax.random.normal(k[2], (IN, R), dtype=jnp.float32) * 0.02
        lora_B = jax.random.normal(k[3], (E, R, OUT), dtype=jnp.float32) * 0.02
        router_w = jax.random.normal(k[4], (E, IN), dtype=jnp.float32) * 0.02
        router_b = jnp.zeros((E,), dtype=jnp.float32)
        return {'x': x, 'base_w': base_w, 'base_b': base_b, 'lora_A': lora_A, 'lora_B': lora_B, 'router_w': router_w, 'router_b': router_b}
    _L0_ffn_in = _L0_ffn_setup()

    def _L1_attn_setup():
        import jax, jax.numpy as jnp
        from jax import lax
        import numpy as np
        B, T, C = (8, 256, 128)
        ATT_SCALE = 1.0
        LN_EPS = 1e-05

        def _layernorm(x, g, b):
            mu = jnp.mean(x, axis=-1, keepdims=True)
            var = jnp.mean(jnp.square(x - mu), axis=-1, keepdims=True)
            return (x - mu) * lax.rsqrt(var + LN_EPS) * g + b

        def _wkv_scan(k, v, td):
            kT = jnp.swapaxes(k, 0, 1)
            vT = jnp.swapaxes(v, 0, 1)

            def step(carry, kv):
                num, den = carry
                kt, vt = kv
                den = den * td + kt
                num = num * td + kt * vt
                return ((num, den), num / (den + 1e-08))
            z = jnp.zeros((k.shape[0], k.shape[2]), dtype=k.dtype)
            _, wkvT = lax.scan(step, (z, z), (kT, vT))
            return jnp.swapaxes(wkvT, 0, 1)

        def _reference_tuple_inner(x, time_decay, time_mix_k, time_mix_v, time_mix_r, Wk, Wv, Wr, Wo, ln_g, ln_b):
            x = _layernorm(x, ln_g, ln_b)
            last_x = jnp.pad(x[:, :-1], ((0, 0), (1, 0), (0, 0)))
            k = (x * time_mix_k + last_x * (1.0 - time_mix_k)) @ Wk.T
            v = (x * time_mix_v + last_x * (1.0 - time_mix_v)) @ Wv.T
            r = (x * time_mix_r + last_x * (1.0 - time_mix_r)) @ Wr.T
            k = k * ATT_SCALE
            td = jnp.exp(time_decay)
            wkv = _wkv_scan(jnp.exp(k), v, td)
            out = jax.nn.sigmoid(r) * wkv @ Wo.T
            new_state = x[:, -1:]
            return (out, new_state)
        key = jax.random.key(seed)
        ks = jax.random.split(key, 10)
        scale = 1.0 / np.sqrt(C)
        x = jax.random.normal(ks[0], (B, T, C), dtype=jnp.float32)
        Wk = jax.random.normal(ks[1], (C, C), dtype=jnp.float32) * scale
        Wv = jax.random.normal(ks[2], (C, C), dtype=jnp.float32) * scale
        Wr = jax.random.normal(ks[3], (C, C), dtype=jnp.float32) * scale
        Wo = jax.random.normal(ks[4], (C, C), dtype=jnp.float32) * scale
        decay_init = jnp.linspace(0.1, 0.45, C, dtype=jnp.float32)
        time_decay = jnp.log(decay_init / (1.0 - decay_init))
        time_mix_k = jax.random.uniform(ks[5], (1, 1, C), dtype=jnp.float32) * 0.375
        time_mix_v = jax.random.uniform(ks[6], (1, 1, C), dtype=jnp.float32) * 0.5
        time_mix_r = jax.random.uniform(ks[7], (1, 1, C), dtype=jnp.float32) * 0.375
        ln_g = jnp.ones((C,), dtype=jnp.float32)
        ln_b = jnp.zeros((C,), dtype=jnp.float32)
        return {'x': x, 'time_decay': time_decay, 'time_mix_k': time_mix_k, 'time_mix_v': time_mix_v, 'time_mix_r': time_mix_r, 'Wk': Wk, 'Wv': Wv, 'Wr': Wr, 'Wo': Wo, 'ln_g': ln_g, 'ln_b': ln_b}
    _L1_attn_in = _L1_attn_setup()

    def _L1_ffn_setup():
        import jax, jax.numpy as jnp
        import numpy as np
        B, S, D, E, K = (2, 256, 128, 8, 2)
        H = 4 * D
        key = jax.random.key(seed)
        ks = jax.random.split(key, 6)
        x = jax.random.normal(ks[0], (B, S, D), dtype=jnp.float32)
        lim_g = np.sqrt(6.0 / (D + E)).astype(np.float32)
        W_gate = jax.random.uniform(ks[1], (D, E), minval=-lim_g, maxval=lim_g, dtype=jnp.float32)
        lim1 = np.sqrt(1.0 / D).astype(np.float32)
        lim2 = np.sqrt(1.0 / H).astype(np.float32)
        W1 = jax.random.uniform(ks[2], (E, D, H), minval=-lim1, maxval=lim1, dtype=jnp.float32)
        b1 = jax.random.uniform(ks[3], (E, H), minval=-lim1, maxval=lim1, dtype=jnp.float32)
        W2 = jax.random.uniform(ks[4], (E, H, D), minval=-lim2, maxval=lim2, dtype=jnp.float32)
        b2 = jax.random.uniform(ks[5], (E, D), minval=-lim2, maxval=lim2, dtype=jnp.float32)
        return {'x': x, 'W_gate': W_gate, 'W1': W1, 'b1': b1, 'W2': W2, 'b2': b2}
    _L1_ffn_in = _L1_ffn_setup()
    _d = {'L0_attn_x': _L0_attn_in['x'], 'L0_attn_qkv_w': _L0_attn_in['qkv_w'], 'L0_attn_qkv_b': _L0_attn_in['qkv_b'], 'L0_attn_out_w': _L0_attn_in['out_w'], 'L0_attn_out_b': _L0_attn_in['out_b'], 'L0_ffn_base_w': _L0_ffn_in['base_w'], 'L0_ffn_base_b': _L0_ffn_in['base_b'], 'L0_ffn_lora_A': _L0_ffn_in['lora_A'], 'L0_ffn_lora_B': _L0_ffn_in['lora_B'], 'L0_ffn_router_w': _L0_ffn_in['router_w'], 'L0_ffn_router_b': _L0_ffn_in['router_b'], 'L1_attn_time_decay': _L1_attn_in['time_decay'], 'L1_attn_time_mix_k': _L1_attn_in['time_mix_k'], 'L1_attn_time_mix_v': _L1_attn_in['time_mix_v'], 'L1_attn_time_mix_r': _L1_attn_in['time_mix_r'], 'L1_attn_Wk': _L1_attn_in['Wk'], 'L1_attn_Wv': _L1_attn_in['Wv'], 'L1_attn_Wr': _L1_attn_in['Wr'], 'L1_attn_Wo': _L1_attn_in['Wo'], 'L1_attn_ln_g': _L1_attn_in['ln_g'], 'L1_attn_ln_b': _L1_attn_in['ln_b'], 'L1_ffn_W_gate': _L1_ffn_in['W_gate'], 'L1_ffn_W1': _L1_ffn_in['W1'], 'L1_ffn_b1': _L1_ffn_in['b1'], 'L1_ffn_W2': _L1_ffn_in['W2'], 'L1_ffn_b2': _L1_ffn_in['b2']}
    _x0 = _d['L0_attn_x']
    _d['L0_attn_x'] = jax.random.normal(jax.random.fold_in(jax.random.key(seed), 1), (8, 512, 128), dtype=_x0.dtype)
    del _x0
    return _d

def reference(L0_attn_x, L0_attn_qkv_w, L0_attn_qkv_b, L0_attn_out_w, L0_attn_out_b, L0_ffn_base_w, L0_ffn_base_b, L0_ffn_lora_A, L0_ffn_lora_B, L0_ffn_router_w, L0_ffn_router_b, L1_attn_time_decay, L1_attn_time_mix_k, L1_attn_time_mix_v, L1_attn_time_mix_r, L1_attn_Wk, L1_attn_Wv, L1_attn_Wr, L1_attn_Wo, L1_attn_ln_g, L1_attn_ln_b, L1_ffn_W_gate, L1_ffn_W1, L1_ffn_b1, L1_ffn_W2, L1_ffn_b2):

    def _L0_attn_ref(x, qkv_w, qkv_b, out_w, out_b):
        import jax, jax.numpy as jnp
        import numpy as np
        D_MODEL = 128
        N_HEADS = 16
        D_HEAD = D_MODEL // N_HEADS
        M_SLOPE = 0.5
        BATCH = 2
        SEQ = 256

        def _alibi_bias(n_heads, seq_len, m, dtype):
            slopes = m ** jnp.arange(n_heads, dtype=dtype)
            pos = jnp.arange(seq_len, dtype=dtype)
            dist = jnp.abs(pos[:, None] - pos[None, :])
            return -dist[None, :, :] * slopes[:, None, None]
        batch, seq_len, d_model = x.shape
        qkv = x @ qkv_w.T + qkv_b
        qkv = qkv.reshape(batch, seq_len, N_HEADS, 3 * D_HEAD).transpose(0, 2, 1, 3)
        q, k, v = jnp.split(qkv, 3, axis=-1)
        scale = jnp.sqrt(jnp.asarray(D_HEAD, dtype=x.dtype))
        scores = jnp.einsum('bhid,bhjd->bhij', q, k) / scale
        scores = scores + _alibi_bias(N_HEADS, seq_len, M_SLOPE, x.dtype)[None]
        attn = jax.nn.softmax(scores, axis=-1)
        out = jnp.einsum('bhij,bhjd->bhid', attn, v)
        out = out.transpose(0, 2, 1, 3).reshape(batch, seq_len, d_model)
        return out @ out_w.T + out_b

    def _L0_ffn_ref(x, base_w, base_b, lora_A, lora_B, router_w, router_b):
        import jax, jax.numpy as jnp
        import numpy as np
        B, S, IN, OUT, E, R = (8, 512, 128, 128, 8, 8)
        LORA_ALPHA = 16
        SCALING = LORA_ALPHA / R
        result = jnp.einsum('bsd,od->bso', x, base_w) + base_b
        logits = jnp.einsum('bsd,ed->bse', x, router_w) + router_b
        gating = jax.nn.softmax(logits, axis=-1).astype(jnp.bfloat16)
        mid = jnp.einsum('bsd,dr->bsr', x, lora_A)
        lora_out = jnp.einsum('bsr,erd,bse->bsd', mid, lora_B, gating.astype(jnp.float32))
        return result + lora_out * SCALING

    def _L1_attn_ref(x, time_decay, time_mix_k, time_mix_v, time_mix_r, Wk, Wv, Wr, Wo, ln_g, ln_b):
        import jax, jax.numpy as jnp
        from jax import lax
        import numpy as np
        B, T, C = (8, 256, 128)
        ATT_SCALE = 1.0
        LN_EPS = 1e-05

        def _layernorm(x, g, b):
            mu = jnp.mean(x, axis=-1, keepdims=True)
            var = jnp.mean(jnp.square(x - mu), axis=-1, keepdims=True)
            return (x - mu) * lax.rsqrt(var + LN_EPS) * g + b

        def _wkv_scan(k, v, td):
            kT = jnp.swapaxes(k, 0, 1)
            vT = jnp.swapaxes(v, 0, 1)

            def step(carry, kv):
                num, den = carry
                kt, vt = kv
                den = den * td + kt
                num = num * td + kt * vt
                return ((num, den), num / (den + 1e-08))
            z = jnp.zeros((k.shape[0], k.shape[2]), dtype=k.dtype)
            _, wkvT = lax.scan(step, (z, z), (kT, vT))
            return jnp.swapaxes(wkvT, 0, 1)

        def _reference_tuple_inner(x, time_decay, time_mix_k, time_mix_v, time_mix_r, Wk, Wv, Wr, Wo, ln_g, ln_b):
            x = _layernorm(x, ln_g, ln_b)
            last_x = jnp.pad(x[:, :-1], ((0, 0), (1, 0), (0, 0)))
            k = (x * time_mix_k + last_x * (1.0 - time_mix_k)) @ Wk.T
            v = (x * time_mix_v + last_x * (1.0 - time_mix_v)) @ Wv.T
            r = (x * time_mix_r + last_x * (1.0 - time_mix_r)) @ Wr.T
            k = k * ATT_SCALE
            td = jnp.exp(time_decay)
            wkv = _wkv_scan(jnp.exp(k), v, td)
            out = jax.nn.sigmoid(r) * wkv @ Wo.T
            new_state = x[:, -1:]
            return (out, new_state)
        return _reference_tuple_inner(x, time_decay, time_mix_k, time_mix_v, time_mix_r, Wk, Wv, Wr, Wo, ln_g, ln_b)[0]

    def _L1_ffn_ref(x, W_gate, W1, b1, W2, b2):
        import jax, jax.numpy as jnp
        import numpy as np
        B, S, D, E, K = (2, 256, 128, 8, 2)
        H = 4 * D
        gate = jnp.einsum('bsd,de->bse', x, W_gate)
        kth = jax.lax.top_k(gate, K)[0][..., -1:]
        mask = jax.nn.softmax(jnp.where(gate >= kth, gate, -jnp.inf), axis=-1)
        h = jax.nn.relu(jnp.einsum('bsd,edh->bseh', x, W1) + b1)
        y = jnp.einsum('bseh,ehd->bsed', h, W2) + b2
        return (y * mask[..., None]).mean(axis=-2)
    x = L0_attn_x
    x = x + _layernorm(_L0_attn_ref(_layernorm(x, axis=-1), L0_attn_qkv_w, L0_attn_qkv_b, L0_attn_out_w, L0_attn_out_b), axis=-1)
    x = x + _layernorm(_L0_ffn_ref(_layernorm(x, axis=-1), L0_ffn_base_w, L0_ffn_base_b, L0_ffn_lora_A, L0_ffn_lora_B, L0_ffn_router_w, L0_ffn_router_b), axis=-1)
    x = x + _layernorm(_L1_attn_ref(_layernorm(x, axis=-1), L1_attn_time_decay, L1_attn_time_mix_k, L1_attn_time_mix_v, L1_attn_time_mix_r, L1_attn_Wk, L1_attn_Wv, L1_attn_Wr, L1_attn_Wo, L1_attn_ln_g, L1_attn_ln_b), axis=-1)
    x = x + _layernorm(_L1_ffn_ref(_layernorm(x, axis=-1), L1_ffn_W_gate, L1_ffn_W1, L1_ffn_b1, L1_ffn_W2, L1_ffn_b2), axis=-1)
    return x

_drawn_inputs = setup_inputs


def setup_inputs(seed=0):
    import zlib

    import numpy as np

    out = dict(_drawn_inputs(seed))
    spreads = {'L0_attn_qkv_b': (0.0, 0.1),
     'L0_attn_out_b': (0.0, 0.1),
     'L0_ffn_base_b': (0.0, 0.1),
     'L0_ffn_router_b': (0.0, 0.73),
     'L1_attn_ln_g': (1.0, 0.2),
     'L1_attn_ln_b': (0.0, 0.1)}
    factors = {'L0_ffn_router_w': 3.288}
    for name, (base, spread) in spreads.items():
        noise = np.random.default_rng([zlib.crc32(name.encode()), seed]).standard_normal(out[name].shape)
        drawn = base * np.exp(spread * noise) if base else spread * noise
        out[name] = jnp.asarray(drawn.astype(out[name].dtype))
    for name, factor in factors.items():
        out[name] = (out[name] * factor).astype(out[name].dtype)
    return out
```

```python
from contextlib import ExitStack

import numpy as np

import concourse.bass as bass
from concourse import mybir

F32 = mybir.dt.float32
BF16 = mybir.dt.bfloat16
ALU = mybir.AluOpType
ACT = mybir.ActivationFunctionType
AX = mybir.AxisListType

P = 128
BATCH, SEQ, D = 8, 512, 128
NT = SEQ // P
HEADS, DH = 16, 8
HG = 4
GROUPS = HEADS // HG
EXPERTS, HID = 8, 512
HB = HID // P
RANK, LORA_E = 8, 8
LORA_SCALE = 16.0 / RANK
EPS = 1e-5
WKV_EPS = 1e-8

SLOTS = [(0, 0), (0, 1), (1, 0), (1, 1), (0, 2), (2, 0)]
BIAS_ROW = DH * len(SLOTS)
MAX_ROW = BIAS_ROW + 3 * NT
CONST_ROWS = 3 * NT + 2

UNITS = HEADS * NT
LEAD = 8
STEPS = GROUPS * NT

BANK_MAX = (0, 1)
BANK_EXP = (2, 3)
BANK_OUT = 4
BANK_A, BANK_B, BANK_C = 5, 6, 7


def at(b, k, of):
    return b * of + k


def layer_norms_attention_lora_wkv_moe_kernel(nc, t):
    ctx = ExitStack()
    with ctx:
        def sb(name, shape, dt=F32):
            return ctx.enter_context(nc.sbuf_tensor(name, shape, dt))

        def sem(name):
            return ctx.enter_context(nc.semaphore(name))

        ps = ctx.enter_context(nc.psum_tensor("ps", [P, 8, SEQ], F32))

        def bank4(n, w=D):
            return ps[:, n, 0:NT * w].rearrange("p (t w) -> p t w", t=NT)

        ident = sb("ident", [P, P])
        identb = sb("identb", [P, P], BF16)
        diag = sb("diag", [P, HEADS, P], BF16)
        wq, wk, wv, wo = (sb(n, [P, D]) for n in ("wq", "wk", "wv", "wo"))
        bq, bk = sb("bq", [P, 1]), sb("bk", [P, 1])
        bv, bo = sb("bv", [P, D]), sb("bo", [P, D])
        w_rm = sb("w_rm", [P, LORA_E + RANK])
        b_route = sb("b_route", [P, LORA_E])
        w_base = sb("w_base", [P, D])
        lora_b = sb("lora_b", [P, D])
        decay, ln_g, ln_b = sb("decay", [P, 1]), sb("ln_g", [P, 1]), sb("ln_b", [P, 1])
        mix_k, mix_v, mix_r = sb("mix_k", [P, 1]), sb("mix_v", [P, 1]), sb("mix_r", [P, 1])
        wkk, wkv_, wkr, wko = (sb(n, [P, D]) for n in ("wkk", "wkv_", "wkr", "wko"))
        w_gate = sb("w_gate", [P, EXPERTS])
        w1 = sb("w1", [P, EXPERTS, HID])
        w2 = sb("w2", [P, EXPERTS * HB, D])
        b1 = sb("b1", [P, EXPERTS * HB])
        neg_b1 = sb("neg_b1", [P, EXPERTS * HB])
        b2x3 = sb("b2x3", [3 * EXPERTS, D])
        pick = sb("pick", [P, EXPERTS, P], BF16)
        b1_col = sb("b1_col", [P, EXPERTS * HB, 3 * EXPERTS])
        skip = sb("skip", [3 * EXPERTS, D])
        skip_rest = sb("skip_rest", [3 * EXPERTS, 2, D])
        skip_parts = sb("skip_parts", [P, 3, D], BF16)
        ones = sb("ones", [P, SEQ])
        td = sb("td", [P, 1])
        free_marks = sb("free_marks", [P, 4])
        td_row = sb("td_row", [P, SEQ])
        minus_half = sb("minus_half", [P, NT])
        eps = sb("eps", [P, NT])

        x_in = sb("x_in", [P, NT, D])
        x_res = sb("x_res", [P, NT, D])
        LN = ("a", "ao", "b", "bo", "c", "co", "d", "do")
        stats = {n: sb(f"stats_{n}", [P, NT, 6]) for n in LN}
        moments = {n: sb(f"moments_{n}", [P, NT, 2]) for n in LN}
        var_eps = {n: sb(f"var_eps_{n}", [P, NT]) for n in LN}
        rstd = {n: sb(f"rstd_{n}", [P, NT]) for n in LN}
        normed = {n: sb(f"normed_{n}", [P, NT, D]) for n in LN}
        h_t = {n: sb(f"h_t_{n}", [P, SEQ]) for n in ("a", "b", "d")}
        qk = [sb(f"qk{i}", [P, SEQ]) for i in range(2)]
        qk_rest = [sb(f"qk_rest{i}", [P, SEQ]) for i in range(2)]
        qk_parts = [sb(f"qk_parts{i}", [P, 3, SEQ], BF16) for i in range(2)]
        q_stack = sb("q_stack", [P, HEADS, SEQ], BF16)
        k_stack = sb("k_stack", [P, HEADS, SEQ], BF16)
        v_aug = sb("v_aug", [P, NT, HEADS, 32])
        maxima = sb("maxima", [P, 2, HG * NT])
        max_hi = sb("max_hi", [HG * NT, 2, P], BF16)
        max_lo = sb("max_lo", [HG * NT, 2, P], BF16)
        probs = sb("probs", [P, 2, HG, SEQ])
        heads_t = sb("heads_t", [P, SEQ])
        inv_sum = sb("inv_sum", [P, NT, HG])
        heads = sb("heads", [P, NT, HEADS, DH])
        heads_all_t = sb("heads_all_t", [P, SEQ])
        attn = sb("attn", [P, NT, D])
        logits = sb("logits", [P, NT, LORA_E])
        route_max = sb("route_max", [P, NT])
        shifted = sb("shifted", [P, NT, LORA_E])
        route_exp = sb("route_exp", [P, NT, LORA_E])
        route_sum = sb("route_sum", [P, NT])
        route_inv = sb("route_inv", [P, NT])
        gating = sb("gating", [P, NT, LORA_E], BF16)
        mid = sb("mid", [P, NT, RANK])
        outer = sb("outer", [P, NT, P])
        outer_t = sb("outer_t", [P, SEQ])
        var1 = sb("var1", [P, NT])
        rstd2 = sb("rstd2", [P, NT])
        rstd12 = sb("rstd12", [P, NT])
        xs_t = sb("xs_t", [P, 1 + SEQ])
        delta = sb("delta", [P, SEQ])
        mixed = [sb(f"mixed{i}", [P, SEQ]) for i in range(3)]
        exp_k = sb("exp_k", [P, SEQ])
        exp_r = sb("exp_r", [P, SEQ])
        kv = sb("kv", [P, SEQ])
        den = sb("den", [P, SEQ])
        num = sb("num", [P, SEQ])
        den_eps = sb("den_eps", [P, SEQ])
        wkv_inv = sb("wkv_inv", [P, SEQ])
        wkv = sb("wkv", [P, SEQ])
        gates = sb("gates", [P, NT, EXPERTS])
        top = sb("top", [P, NT, 8])
        chosen = sb("chosen", [P, NT, EXPERTS])
        gate_sh = sb("gate_sh", [P, NT, EXPERTS])
        gate_exp = sb("gate_exp", [P, NT, EXPERTS])
        gate_kept = sb("gate_kept", [P, NT, EXPERTS])
        gate_sum = sb("gate_sum", [P, NT])
        gate_inv = sb("gate_inv", [P, NT])
        share = sb("share", [P, NT, EXPERTS])
        share_rest = sb("share_rest", [P, NT, EXPERTS])
        share_parts = sb("share_parts", [P, NT, P], BF16)
        share_t = sb("share_t", [P, SEQ], BF16)
        share_row = sb("share_row", [P, 2, SEQ])
        hidden = sb("hidden", [P, 2, SEQ])
        moe_t = sb("moe_t", [P, SEQ])
        result = sb("result", [P, NT, D])

        names = [f"{a}_{n}" for n in LN for a in ("stats", "moments", "vareps", "rstd", "normed")]
        names += """loaded cleared consts_ready skip_mm skip_sum skip_hi skip_rest skip_done td_done
            x_loaded out_stored res_a res_b res_c res_d
            ht_a_mm ht_a qk_mm v_mm qk_scaled qk_hi qk_rest1 qk_mid qk_lo v_done parts_stored
            stacks_loaded s1_ready s1_used max_mm max_hi_s max_lo_s mrow0 mrow1
            s2_ready probs_done pv_done ov_done heads_t_s heads_mm inv_s heads_s heads_all_mm heads_all_s
            attn_mm attn_s
            ht_b_mm ht_b rm_mm logits_s rmax_s rshift_s rexp_s rsum_s rinv_s gating_s mid_s outer_s
            outer_mm outer_t_s lora_mm
            c_var1 c_vareps2 c_rstd2 xs_mm xs_s delta_s mix_s wkv_k_mm wkv_v_mm wkv_r_mm expk_s expr_s kv_s
            den_s num_s deneps_s denr_s winv_s wkv_s wkvo_mm
            ht_d_mm ht_d gate_mm gates_s top_s chosen_s gshift_s gexp_s gkept_s gsum_s ginv_s share_s
            shi_s srest_s smid_s slo_s share_mm share_t_s row_mm row_s z_mm hidden_s y_mm y_s yt_mm
            """.split()
        S = {n: sem(n) for n in names}

        block = ctx.enter_context(nc.Block())

        loads = [
            (ident[:], t["ident"]), (identb[:], t["identb"]), (diag[:], t["diag"]),
            (wq[:], t["wq"]), (wk[:], t["wk"]), (wv[:], t["wv"]), (wo[:], t["wo"]),
            (bq[:], t["bq"]), (bk[:], t["bk"]),
            (bv[:], t["bv"].partition_broadcast(P)), (bo[:], t["bo"].partition_broadcast(P)),
            (w_rm[:, 0:LORA_E], t["route_w"]), (w_rm[:, LORA_E:], t["lora_a"]),
            (b_route[:], t["route_b"].partition_broadcast(P)), (w_base[:], t["base_w"]),
            (decay[:], t["decay"]), (ln_g[:], t["ln_g"]), (ln_b[:], t["ln_b"]),
            (mix_k[:], t["mix_k"]), (mix_v[:], t["mix_v"]), (mix_r[:], t["mix_r"]),
            (wkk[:], t["wkk"]), (wkv_[:], t["wkv"]), (wkr[:], t["wkr"]), (wko[:], t["wko"]),
            (w_gate[:], t["w_gate"]), (b1[:], t["b1"]),
            (b2x3[0:8, :], t["b2"]), (b2x3[8:16, :], t["b2"]), (b2x3[16:24, :], t["b2"]),
            (pick[:], t["pick"]),
            (w1[:], t["w1"].rearrange("e d h -> d e h")),
            (w2[:], t["w2"].rearrange("e (n p) d -> p (e n) d", p=P)),
        ]
        late_loads = [
            (q_stack[BIAS_ROW:BIAS_ROW + CONST_ROWS, :, :], t["q_rows"]),
            (k_stack[BIAS_ROW:BIAS_ROW + CONST_ROWS, :, :], t["k_rows"]),
            (lora_b[0:LORA_E * RANK, :], t["lora_b"]), (lora_b[LORA_E * RANK:LORA_E * RANK + 1, :], t["base_b"]),
        ]
        LOADED = 16 * (len(loads) + len(late_loads))
        SLOT_DMAS = 2 * len(SLOTS) + 1
        CLEARS = 2

        def unit(u):
            return u // (HG * NT), u // NT % HG + u // (HG * NT) * HG, u % NT

        @block.sync
        def _(sp):
            for dst, src in loads:
                sp.dma_start(dst, src).then_inc(S["loaded"], 16)
            sp.wait_ge(S["cleared"], CLEARS)
            for dst, src in late_loads:
                sp.dma_start(dst, src).then_inc(S["loaded"], 16)

            def load_x(b):
                sp.wait_ge(S["res_a"], at(b, 1, 1))
                sp.dma_start(x_in[:], t["x"][bass.ds(b, 1), :, :].rearrange("o (t p) d -> p (o t) d", p=P)
                             ).then_inc(S["x_loaded"], 16)

            def build_stacks(b):
                for i, n in ((0, 1), (1, 2)):
                    sp.wait_ge(S["qk_lo"], at(b, n, 2))
                    sp.wait_ge(S["qk_mid"], at(b, n, 2))
                    sp.dma_start(t["parts"][i].rearrange("k p n -> p k n"), qk_parts[i][:]
                                 ).then_inc(S["parts_stored"], 16)
                sp.wait_ge(S["parts_stored"], at(b, 1, 1) * 32)
                for s, pair in enumerate(SLOTS):
                    for i, stack in ((0, q_stack), (1, k_stack)):
                        sp.dma_start(stack[DH * s:DH * s + DH, :, :],
                                     t["parts"][i, pair[i]].rearrange("(h d) n -> d h n", d=DH)
                                     ).then_inc(S["stacks_loaded"], 16)
                sp.dma_start(q_stack[MAX_ROW:MAX_ROW + 2, :, :], t["q_rows"][3 * NT:3 * NT + 2]
                             ).then_inc(S["stacks_loaded"], 16)

            def max_rows(b, g):
                dst = q_stack[:, HG * g:HG * g + HG, :]
                sp.wait_ge(S["max_lo_s"], at(b, g + 1, GROUPS))
                for k, src in ((0, max_hi), (1, max_lo)):
                    sp.dma_start(dst[MAX_ROW + k:MAX_ROW + k + 1].rearrange("p h (i c) -> p (h i) c", c=P),
                                 src[:, g % 2, :]).then_inc(S[f"mrow{g % 2}"], 16)

            def store(b):
                sp.wait_ge(S["res_d"], at(b, 1, 1))
                sp.dma_start(t["out"][bass.ds(b, 1), :, :].rearrange("o (t p) d -> p (o t) d", p=P), result[:]
                             ).then_inc(S["out_stored"], 16)

            with sp.Fori(0, BATCH) as b:
                load_x(b)
                build_stacks(b)
                for g in range(GROUPS):
                    max_rows(b, g)
                store(b)
            sp.wait_ge(S["out_stored"], 16 * (BATCH + 1))

        @block.gpsimd
        def _(pool):
            pool.memset(q_stack[:], 0.0)
            pool.memset(k_stack[:], 0.0)
            pool.memset(lora_b[:], 0.0).then_inc(S["cleared"], 1)
            pool.memset(v_aug[:], 0.0)
            pool.memset(share_parts[:], 0.0)
            pool.memset(outer[:], 0.0)
            pool.memset(skip_parts[:], 0.0)
            pool.memset(b1_col[:], 0.0)
            pool.memset(minus_half[:], -0.5)
            pool.memset(eps[:], EPS)
            pool.memset(xs_t[:, 0:1], 0.0).then_inc(S["cleared"], 1)
            pool.wait_ge(S["cleared"], 2)

            def rsqrt(b, n):
                pool.wait_ge(S[f"moments_{n}"], at(b, 1, 1))
                pool.tensor_tensor(var_eps[n][:], moments[n][:, :, 1], eps[:], ALU.add
                                   ).then_inc(S[f"vareps_{n}"], 1)
                pool.wait_ge(S[f"vareps_{n}"], at(b, 1, 1))
                pool.tensor_tensor(rstd[n][:], var_eps[n][:], minus_half[:], ALU.pow
                                   ).then_inc(S[f"rstd_{n}"], 1)

            def rsqrt_twice(b):
                pool.wait_ge(S["rstd_c"], at(b, 1, 1))
                pool.tensor_tensor(var1[:], moments["c"][:, :, 1], rstd["c"][:], ALU.mult).then_inc(S["c_var1"], 1)
                pool.wait_ge(S["c_var1"], at(b, 1, 2))
                pool.tensor_tensor(var1[:], var1[:], rstd["c"][:], ALU.mult).then_inc(S["c_var1"], 1)
                pool.wait_ge(S["c_var1"], at(b, 2, 2))
                pool.tensor_tensor(var1[:], var1[:], eps[:], ALU.add).then_inc(S["c_vareps2"], 1)
                pool.wait_ge(S["c_vareps2"], at(b, 1, 1))
                pool.tensor_tensor(rstd2[:], var1[:], minus_half[:], ALU.pow).then_inc(S["c_rstd2"], 1)
                pool.wait_ge(S["c_rstd2"], at(b, 1, 2))
                pool.tensor_tensor(rstd12[:], rstd2[:], rstd["c"][:], ALU.mult).then_inc(S["c_rstd2"], 1)

            def split(b):
                for i in range(2):
                    pool.wait_ge(S["qk_hi"], at(b, i + 1, 2))
                    pool.tensor_tensor(qk_rest[i][:], qk[i][:], qk_parts[i][:, 0, :], ALU.subtract
                                       ).then_inc(S["qk_rest1"], 1)
                for i in range(2):
                    pool.wait_ge(S["qk_mid"], at(b, i + 1, 2))
                    pool.tensor_tensor(qk_parts[i][:, 2, :], qk_rest[i][:], qk_parts[i][:, 1, :], ALU.subtract
                                       ).then_inc(S["qk_lo"], 1)

            with pool.Fori(0, BATCH) as b:
                rsqrt(b, "a")
                split(b)
                rsqrt(b, "ao")
                rsqrt(b, "b")
                rsqrt(b, "bo")
                rsqrt(b, "c")
                rsqrt_twice(b)
                rsqrt(b, "co")
                rsqrt(b, "d")
                rsqrt(b, "do")

        @block.scalar
        def _(act):
            act.wait_ge(S["loaded"], LOADED)
            act.activation(td[:], decay[:], ACT.Exp).then_inc(S["td_done"], 1)

            def transposed(b, n):
                act.wait_ge(S[f"ht_{n}_mm"], at(b, 1, 1))
                act.activation(h_t[n][:], ps[:, {"a": BANK_A, "b": BANK_B, "d": BANK_C}[n], :], ACT.Copy
                               ).then_inc(S[f"ht_{n}"], 1)

            def split(b):
                for i in range(2):
                    act.wait_ge(S["qk_scaled"], at(b, i + 1, 2))
                    act.activation(qk_parts[i][:, 0, :], qk[i][:], ACT.Copy).then_inc(S["qk_hi"], 1)
                for i in range(2):
                    act.wait_ge(S["qk_rest1"], at(b, i + 1, 2))
                    act.activation(qk_parts[i][:, 1, :], qk_rest[i][:], ACT.Copy).then_inc(S["qk_mid"], 1)

            def exps(b, s):
                if s >= 2:
                    act.wait_ge(S["pv_done"], at(b, s - 1, STEPS))
                for h in range(HG):
                    n = HG * s + h
                    act.wait_ge(S["s2_ready"], at(b, n + 1, UNITS))
                    act.activation(probs[:, s % 2, h, :], ps[:, BANK_EXP[n % 2], :], ACT.Exp
                                   ).then_inc(S["probs_done"], 1)

            def head_out(b, g):
                act.wait_ge(S["pv_done"], at(b, NT * (g + 1), STEPS))
                act.activation(heads_t[:], ps[:, BANK_OUT, :], ACT.Copy).then_inc(S["heads_t_s"], 1)

            def heads_transposed(b):
                act.wait_ge(S["heads_all_mm"], at(b, 1, 1))
                act.activation(heads_all_t[:], ps[:, BANK_B, :], ACT.Copy).then_inc(S["heads_all_s"], 1)

            def lora(b):
                transposed(b, "b")
                act.wait_ge(S["rshift_s"], at(b, 1, 1))
                act.activation(route_exp[:], shifted[:], ACT.Exp).then_inc(S["rexp_s"], 1)
                act.wait_ge(S["outer_mm"], at(b, 1, 1))
                act.activation(outer_t[:], ps[:, BANK_C, :], ACT.Copy).then_inc(S["outer_t_s"], 1)

            def time_mix(b):
                act.wait_ge(S["xs_mm"], at(b, 1, 1))
                act.activation(xs_t[:, 1:], ps[:, BANK_B, :], ACT.Identity, bias=ln_b[:], scale=ln_g[:]
                               ).then_inc(S["xs_s"], 1)
                act.wait_ge(S["wkv_k_mm"], at(b, 1, 1))
                act.activation(exp_k[:], ps[:, BANK_C, :], ACT.Exp).then_inc(S["expk_s"], 1)
                act.wait_ge(S["wkv_r_mm"], at(b, 1, 1))
                act.activation(exp_r[:], ps[:, BANK_C, :], ACT.Exp, scale=-1.0).then_inc(S["expr_s"], 1)

            def moe_gate(b):
                transposed(b, "d")
                act.wait_ge(S["gshift_s"], at(b, 1, 1))
                act.activation(gate_exp[:], gate_sh[:], ACT.Exp).then_inc(S["gexp_s"], 1)
                act.wait_ge(S["share_mm"], at(b, 1, 1))
                act.activation(share_t[:], ps[:, BANK_B, :].bitcast(BF16)[:, 0:SEQ], ACT.Copy
                               ).then_inc(S["share_t_s"], 1)

            def share_rows(b, e):
                act.wait_ge(S["row_mm"], at(b, e + 1, EXPERTS))
                if e >= 2:
                    act.wait_ge(S["hidden_s"], at(b, HB * (e - 1), EXPERTS * HB))
                act.activation(share_row[:, e % 2, :], ps[:, BANK_EXP[e % 2], :], ACT.Copy
                               ).then_inc(S["row_s"], 1)

            with act.Fori(0, BATCH) as b:
                transposed(b, "a")
                split(b)
                for s in range(STEPS):
                    exps(b, s)
                    if s % NT == 1 and s > NT:
                        head_out(b, s // NT - 1)
                head_out(b, GROUPS - 1)
                heads_transposed(b)
                lora(b)
                time_mix(b)
                moe_gate(b)
                for e in range(EXPERTS):
                    share_rows(b, e)
                act.wait_ge(S["y_mm"], at(b, 1, 1))
                act.activation(moe_t[:], ps[:, BANK_OUT, :], ACT.Copy).then_inc(S["y_s"], 1)

        @block.tensor
        def _(pe):
            pe.wait_ge(S["loaded"], LOADED)
            pe.wait_ge(S["cleared"], 2)

            def mm(out, lhs, rhs, start=True, stop=True, **kw):
                return pe.matmul(out, lhs, rhs, start=start, stop=stop, skip_group_check=True, **kw)

            pe.wait_ge(S["consts_ready"], 1)
            for n in range(EXPERTS * HB):
                last = mm(ps[0:3 * EXPERTS, BANK_A, 0:D], b1_col[:, n, :], w2[:, n, :],
                          start=(n == 0), stop=(n == EXPERTS * HB - 1))
            last.then_inc(S["skip_mm"], 1)

            def transposes(b, n, bank, done):
                pe.wait_ge(S[f"normed_{n}"], at(b, 1, 1))
                for i in range(NT):
                    last = pe.transpose(ps[:, bank, i * P:(i + 1) * P], normed[n][:, i, :], ident[:])
                last.then_inc(S[done], 1)

            def project(b):
                pe.wait_ge(S["ht_a"], at(b, 1, 1))
                mm(ps[:, BANK_B, :], wq[:], h_t["a"][:]).then_inc(S["qk_mm"], 1)
                mm(ps[:, BANK_C, :], wk[:], h_t["a"][:]).then_inc(S["qk_mm"], 1)
                for i in range(NT):
                    last = mm(ps[:, BANK_A, i * D:(i + 1) * D], h_t["a"][:, i * P:(i + 1) * P], wv[:])
                last.then_inc(S["v_mm"], 1)

            def score_max(b, u):
                _, h, i = unit(u)
                bank = ps[:, BANK_MAX[u % 2], :]
                pe.wait_ge(S["s1_used"], at(b, u + 1, UNITS))
                mm(bank, q_stack[:, h, i * P:(i + 1) * P], k_stack[:, h, :], stop=False)
                mm(bank[:, i * P:(i + 1) * P], identb[:], diag[:, h, :], start=False
                   ).then_inc(S["s1_ready"], 1)

            def max_transpose(b, g):
                pe.wait_ge(S["s1_used"], at(b, 2 + (g + 1) * HG * NT, UNITS))
                pe.transpose(ps[0:HG * NT, BANK_A, 0:P], maxima[:, g % 2, :], ident[:]).then_inc(S["max_mm"], 1)

            def score_exp(b, s, h4):
                g, j = s // NT, s % NT
                h, n = HG * g + h4, HG * s + h4
                if j == 0 and h4 == 0:
                    pe.wait_ge(S[f"mrow{g % 2}"], at(b, g // 2 + 1, GROUPS // 2) * 32)
                pe.wait_ge(S["probs_done"], at(b, n + 1, UNITS))
                bank = ps[:, BANK_EXP[n % 2], :]
                mm(bank, k_stack[:, h, j * P:(j + 1) * P], q_stack[:, h, :], stop=False)
                mm(bank[:, j * P:(j + 1) * P], identb[:], diag[:, h, :], start=False
                   ).then_inc(S["s2_ready"], 1)

            def weigh_values(b, s):
                g, j = s // NT, s % NT
                pe.wait_ge(S["probs_done"], at(b, 2 + HG * (s + 1), UNITS))
                if j == 0 and g > 0:
                    pe.wait_ge(S["heads_t_s"], at(b, g, GROUPS))
                for r in range(HG):
                    last = mm(ps[32 * r:32 * r + 32, BANK_OUT, :], v_aug[:, j, HG * g + r, :],
                              probs[:, s % 2, r, :], start=(j == 0), stop=(j == NT - 1), tile_position=(0, 32 * r))
                last.then_inc(S["pv_done"], 1)

            def head_transpose(b, g):
                pe.wait_ge(S["heads_t_s"], at(b, g + 1, GROUPS))
                if g > 0:
                    pe.wait_ge(S["heads_s"], at(b, g, GROUPS))
                for i in range(NT):
                    last = pe.transpose(ps[:, BANK_B, i * P:(i + 1) * P], heads_t[:, i * P:(i + 1) * P], ident[:])
                last.then_inc(S["heads_mm"], 1)

            def attention(b):
                pe.wait_ge(S["stacks_loaded"], at(b, 1, 1) * 16 * SLOT_DMAS)
                pe.wait_ge(S["v_done"], at(b, 1, 1))
                for u in range(HG * NT + LEAD // 2):
                    score_max(b, u)
                max_transpose(b, 0)
                for u in range(HG * NT + LEAD // 2, HG * NT + LEAD):
                    score_max(b, u)
                for s in range(STEPS):
                    for h4 in range(HG):
                        u = HG * NT + LEAD + HG * s + h4
                        if u < UNITS:
                            score_max(b, u)
                        score_exp(b, s, h4)
                    if s > 0:
                        weigh_values(b, s - 1)
                    if s % NT == 2 and s // NT + 1 < GROUPS:
                        max_transpose(b, s // NT + 1)
                    if s % NT == 2 and s > NT:
                        head_transpose(b, s // NT - 1)
                weigh_values(b, STEPS - 1)
                head_transpose(b, GROUPS - 1)
                pe.wait_ge(S["heads_s"], at(b, GROUPS, GROUPS))
                for i in range(NT):
                    last = pe.transpose(ps[:, BANK_B, i * P:(i + 1) * P],
                                        heads[:, i, :, :].rearrange("p h d -> p (h d)"), ident[:])
                last.then_inc(S["heads_all_mm"], 1)
                pe.wait_ge(S["heads_all_s"], at(b, 1, 1))
                for i in range(NT):
                    last = mm(ps[:, BANK_A, i * D:(i + 1) * D], heads_all_t[:, i * P:(i + 1) * P], wo[:])
                last.then_inc(S["attn_mm"], 1)

            def lora(b):
                transposes(b, "b", BANK_B, "ht_b_mm")
                pe.wait_ge(S["ht_b"], at(b, 1, 1))
                for i in range(NT):
                    last = mm(ps[:, BANK_C, i * 16:(i + 1) * 16], h_t["b"][:, i * P:(i + 1) * P], w_rm[:])
                last.then_inc(S["rm_mm"], 1)
                pe.wait_ge(S["outer_s"], at(b, 1, 1))
                for i in range(NT):
                    last = pe.transpose(ps[:, BANK_C, i * P:(i + 1) * P], outer[:, i, :], ident[:])
                last.then_inc(S["outer_mm"], 1)
                pe.wait_ge(S["outer_t_s"], at(b, 1, 1))
                for i in range(NT):
                    out = ps[:, BANK_B, i * D:(i + 1) * D]
                    mm(out, h_t["b"][:, i * P:(i + 1) * P], w_base[:], stop=False)
                    last = mm(out, outer_t[:, i * P:(i + 1) * P], lora_b[:], start=False)
                last.then_inc(S["lora_mm"], 1)

            def time_mix(b):
                transposes(b, "c", BANK_B, "xs_mm")
                pe.wait_ge(S["mix_s"], at(b, 1, 3))
                mm(ps[:, BANK_C, :], wkk[:], mixed[0][:]).then_inc(S["wkv_k_mm"], 1)
                pe.wait_ge(S["mix_s"], at(b, 2, 3))
                mm(ps[:, BANK_B, :], wkv_[:], mixed[1][:]).then_inc(S["wkv_v_mm"], 1)
                pe.wait_ge(S["mix_s"], at(b, 3, 3))
                pe.wait_ge(S["expk_s"], at(b, 1, 1))
                mm(ps[:, BANK_C, :], wkr[:], mixed[2][:]).then_inc(S["wkv_r_mm"], 1)
                pe.wait_ge(S["wkv_s"], at(b, 1, 1))
                for i in range(NT):
                    last = mm(ps[:, BANK_B, i * D:(i + 1) * D], wkv[:, i * P:(i + 1) * P], wko[:])
                last.then_inc(S["wkvo_mm"], 1)

            def experts(b):
                transposes(b, "d", BANK_C, "ht_d_mm")
                pe.wait_ge(S["ht_d"], at(b, 1, 1))
                for i in range(NT):
                    last = mm(ps[:, BANK_B, i * EXPERTS:(i + 1) * EXPERTS], h_t["d"][:, i * P:(i + 1) * P], w_gate[:])
                last.then_inc(S["gate_mm"], 1)
                pe.wait_ge(S["slo_s"], at(b, 1, 1))
                pe.wait_ge(S["smid_s"], at(b, 1, 1))
                shares = ps[:, BANK_B, :].bitcast(BF16)
                for i in range(NT):
                    last = pe.transpose(shares[:, i * P:(i + 1) * P], share_parts[:, i, :], identb[:])
                last.then_inc(S["share_mm"], 1)

                def row(e):
                    if e >= 2:
                        pe.wait_ge(S["row_s"], at(b, e - 1, EXPERTS))
                    mm(ps[:, BANK_EXP[e % 2], :], pick[:, e, :], share_t[:]).then_inc(S["row_mm"], 1)

                def up(n):
                    e, k = n // HB, n % HB
                    if n >= 2:
                        pe.wait_ge(S["hidden_s"], at(b, n - 1, EXPERTS * HB))
                    mm(ps[:, BANK_MAX[n % 2], :], w1[:, e, k * P:(k + 1) * P], h_t["d"][:]).then_inc(S["z_mm"], 1)

                def down(n):
                    pe.wait_ge(S["hidden_s"], at(b, n + 1, EXPERTS * HB))
                    return mm(ps[:, BANK_OUT, :], w2[:, n, :], hidden[:, n % 2, :], start=False,
                              stop=(n == EXPERTS * HB - 1))

                pe.wait_ge(S["share_t_s"], at(b, 1, 1))
                row(0)
                up(0)
                for k in range(3):
                    mm(ps[:, BANK_OUT, :], skip_parts[:, k, :], share_t[:], start=(k == 0), stop=False)
                for n in range(1, EXPERTS * HB):
                    if n % HB == 1 and n // HB + 1 < EXPERTS:
                        row(n // HB + 1)
                    up(n)
                    last = down(n - 1)
                down(EXPERTS * HB - 1).then_inc(S["y_mm"], 1)
                pe.wait_ge(S["y_s"], at(b, 1, 1))
                for i in range(NT):
                    last = pe.transpose(ps[:, BANK_C, i * P:(i + 1) * P], moe_t[:, i * P:(i + 1) * P], ident[:])
                last.then_inc(S["yt_mm"], 1)

            pe.wait_ge(S["skip_done"], 1)
            with pe.Fori(0, BATCH) as b:
                transposes(b, "a", BANK_A, "ht_a_mm")
                project(b)
                attention(b)
                lora(b)
                time_mix(b)
                experts(b)

        @block.vector
        def _(dve):
            dve.wait_ge(S["loaded"], LOADED)
            dve.wait_ge(S["cleared"], 2)
            dve.memset(ones[:], 1.0)
            dve.memset(v_aug[:, :, :, DH:DH + 1], 1.0)
            dve.memset(outer[:, :, LORA_E * RANK:LORA_E * RANK + 1], 1.0)
            dve.tensor_scalar(neg_b1[:], b1[:], -1.0, None, ALU.mult)
            for k in range(3):
                for e in range(EXPERTS):
                    last = dve.tensor_copy(b1_col[:, e * HB:(e + 1) * HB, k * EXPERTS + e], b1[:, e * HB:(e + 1) * HB])
            last.then_inc(S["consts_ready"], 1)
            dve.wait_ge(S["consts_ready"], 1)
            dve.wait_ge(S["td_done"], 1)
            dve.tensor_scalar(td_row[:], ones[:], td[:], None, ALU.mult).then_inc(S["consts_ready"], 1)
            dve.wait_ge(S["skip_mm"], 1)
            R = 3 * EXPERTS
            dve.tensor_tensor(skip[:], ps[0:R, BANK_A, 0:D], b2x3[:], ALU.add).then_inc(S["skip_sum"], 1)
            dve.wait_ge(S["skip_sum"], 1)
            dve.tensor_copy(skip_parts[0:R, 0, :], skip[:]).then_inc(S["skip_hi"], 1)
            dve.wait_ge(S["skip_hi"], 1)
            dve.tensor_tensor(skip_rest[:, 0, :], skip[:], skip_parts[0:R, 0, :], ALU.subtract).then_inc(S["skip_rest"], 1)
            dve.wait_ge(S["skip_rest"], 1)
            dve.tensor_copy(skip_parts[0:R, 1, :], skip_rest[:, 0, :]).then_inc(S["skip_hi"], 1)
            dve.wait_ge(S["skip_hi"], 2)
            dve.tensor_tensor(skip_parts[0:R, 2, :], skip_rest[:, 0, :], skip_parts[0:R, 1, :], ALU.subtract
                              ).then_inc(S["skip_done"], 1)
            dve.memset(maxima[:], 0.0).then_inc(S["s1_used"], 2)
            dve.memset(free_marks[:, 0:1], 1.0).then_inc(S["probs_done"], 2)
            dve.memset(free_marks[:, 1:2], 1.0).then_inc(S["res_a"], 1)
            dve.memset(free_marks[:, 2:3], 1.0).then_inc(S["out_stored"], 16)

            def norm_stats(b, n, src):
                for i in range(NT):
                    last = dve.bn_stats(stats[n][:, i, :], src[:, i, :])
                last.then_inc(S[f"stats_{n}"], 1)
                dve.wait_ge(S["loaded"], LOADED)
                dve.wait_ge(S[f"stats_{n}"], at(b, 1, 1))
                for i in range(NT):
                    last = dve.bn_aggr(moments[n][:, i, :], stats[n][:, i, :])
                last.then_inc(S[f"moments_{n}"], 1)

            def normalize(b, n, src, scale=None, ready=None):
                if ready is None:
                    scale = rstd[n]
                    dve.wait_ge(S[f"rstd_{n}"], at(b, 1, 1))
                else:
                    dve.wait_ge(*ready)
                for i in range(NT):
                    last = dve.tensor_scalar(normed[n][:, i, :], src[:, i, :], moments[n][:, i, 0:1],
                                             scale[:, i:i + 1], ALU.subtract, ALU.mult)
                last.then_inc(S[f"normed_{n}"], 1)

            def add_residual(b, n, base, out, done):
                dve.wait_ge(S[f"normed_{n}"], at(b, 1, 1))
                dve.tensor_tensor(out[:], base[:], normed[n][:], ALU.add).then_inc(S[done], 1)
                dve.wait_ge(S[done], at(b, 1, 1))

            def qkv(b):
                dve.wait_ge(S["qk_mm"], at(b, 1, 2))
                dve.tensor_scalar(qk[0][:], ps[:, BANK_B, :], bq[:], float(DH) ** -0.5, ALU.add, ALU.mult
                                  ).then_inc(S["qk_scaled"], 1)
                dve.wait_ge(S["qk_mm"], at(b, 2, 2))
                dve.tensor_scalar(qk[1][:], ps[:, BANK_C, :], bk[:], None, ALU.add).then_inc(S["qk_scaled"], 1)
                dve.wait_ge(S["v_mm"], at(b, 1, 1))
                for i in range(NT):
                    last = dve.tensor_tensor(v_aug[:, i, :, 0:DH],
                                             ps[:, BANK_A, i * D:(i + 1) * D].rearrange("p (h d) -> p h d", d=DH),
                                             bv[:].rearrange("p (h d) -> p h d", d=DH), ALU.add)
                last.then_inc(S["v_done"], 1)

            def row_max(b, u):
                g = u // (HG * NT)
                dve.wait_ge(S["s1_ready"], at(b, u + 1, UNITS))
                dve.tensor_reduce(maxima[:, g % 2, u % (HG * NT):u % (HG * NT) + 1], ps[:, BANK_MAX[u % 2], :],
                                  AX.X, ALU.max).then_inc(S["s1_used"], 1)

            def max_parts(b, g):
                src = ps[0:HG * NT, BANK_A, 0:P]
                dve.wait_ge(S["max_mm"], at(b, g + 1, GROUPS))
                if g >= 2:
                    dve.wait_ge(S[f"mrow{g % 2}"], at(b, g // 2, GROUPS // 2) * 32)
                dve.tensor_scalar(max_hi[:, g % 2, :], src, -1.0, None, ALU.mult).then_inc(S["max_hi_s"], 1)
                dve.wait_ge(S["max_hi_s"], at(b, g + 1, GROUPS))
                dve.scalar_tensor_tensor(max_lo[:, g % 2, :], src, -1.0, max_hi[:, g % 2, :], ALU.mult, ALU.subtract
                                         ).then_inc(S["max_lo_s"], 1)

            def head_norm(b, g):
                cols = bank4(BANK_B).rearrange("p t (h c) -> p t h c", c=32)
                dve.wait_ge(S["heads_mm"], at(b, g + 1, GROUPS))
                dve.reciprocal(inv_sum[:], cols[:, :, :, DH]).then_inc(S["inv_s"], 1)
                dve.wait_ge(S["inv_s"], at(b, g + 1, GROUPS))
                dve.tensor_tensor(heads[:, :, HG * g:HG * g + HG, :], cols[:, :, :, 0:DH],
                                  inv_sum[:].unsqueeze(3).to_broadcast([P, NT, HG, DH]), ALU.mult
                                  ).then_inc(S["heads_s"], 1)

            def attention(b):
                for u in range(HG * NT + LEAD // 2):
                    row_max(b, u)
                max_parts(b, 0)
                for u in range(HG * NT + LEAD // 2, HG * NT + LEAD):
                    row_max(b, u)
                for s in range(STEPS):
                    for h4 in range(HG):
                        u = HG * NT + LEAD + HG * s + h4
                        if u < UNITS:
                            row_max(b, u)
                    if s % NT == 2 and s // NT + 1 < GROUPS:
                        max_parts(b, s // NT + 1)
                    if s % NT == 2 and s > NT:
                        head_norm(b, s // NT - 1)
                head_norm(b, GROUPS - 1)
                dve.wait_ge(S["attn_mm"], at(b, 1, 1))
                for i in range(NT):
                    last = dve.tensor_tensor(attn[:, i, :], ps[:, BANK_A, i * D:(i + 1) * D], bo[:], ALU.add)
                last.then_inc(S["attn_s"], 1)
                dve.wait_ge(S["attn_s"], at(b, 1, 1))
                norm_stats(b, "ao", attn)
                normalize(b, "ao", attn)
                dve.wait_ge(S["normed_ao"], at(b, 1, 1))
                dve.tensor_tensor(x_res[:], x_in[:], normed["ao"][:], ALU.add).then_inc(S["res_a"], 1)
                dve.wait_ge(S["res_a"], at(b, 2, 1))

            def lora(b):
                norm_stats(b, "b", x_res)
                normalize(b, "b", x_res)
                rm = ps[:, BANK_C, 0:64].rearrange("p (t c) -> p t c", t=NT)
                dve.wait_ge(S["rm_mm"], at(b, 1, 1))
                dve.tensor_tensor(logits[:], rm[:, :, 0:LORA_E],
                                  b_route[:].unsqueeze(1).to_broadcast([P, NT, LORA_E]), ALU.add
                                  ).then_inc(S["logits_s"], 1)
                dve.tensor_scalar(mid[:], rm[:, :, LORA_E:], LORA_SCALE, None, ALU.mult).then_inc(S["mid_s"], 1)
                dve.wait_ge(S["logits_s"], at(b, 1, 1))
                dve.tensor_reduce(route_max[:], logits[:], AX.X, ALU.max).then_inc(S["rmax_s"], 1)
                dve.wait_ge(S["rmax_s"], at(b, 1, 1))
                dve.tensor_tensor(shifted[:], logits[:], route_max[:].unsqueeze(2).to_broadcast([P, NT, LORA_E]),
                                  ALU.subtract).then_inc(S["rshift_s"], 1)
                dve.wait_ge(S["rexp_s"], at(b, 1, 1))
                dve.tensor_reduce(route_sum[:], route_exp[:], AX.X, ALU.add).then_inc(S["rsum_s"], 1)
                dve.wait_ge(S["rsum_s"], at(b, 1, 1))
                dve.reciprocal(route_inv[:], route_sum[:]).then_inc(S["rinv_s"], 1)
                dve.wait_ge(S["rinv_s"], at(b, 1, 1))
                dve.tensor_tensor(gating[:], route_exp[:], route_inv[:].unsqueeze(2).to_broadcast([P, NT, LORA_E]),
                                  ALU.mult).then_inc(S["gating_s"], 1)
                dve.wait_ge(S["gating_s"], at(b, 1, 1))
                products = outer[:, :, 0:LORA_E * RANK].rearrange("p t (e r) -> p t e r", r=RANK)
                dve.tensor_tensor(products, gating[:].unsqueeze(3).to_broadcast([P, NT, LORA_E, RANK]),
                                  mid[:].unsqueeze(2).to_broadcast([P, NT, LORA_E, RANK]), ALU.mult
                                  ).then_inc(S["outer_s"], 1)
                dve.wait_ge(S["lora_mm"], at(b, 1, 1))
                norm_stats(b, "bo", bank4(BANK_B))
                normalize(b, "bo", bank4(BANK_B))
                add_residual(b, "bo", x_res, x_res, "res_b")

            def time_mix(b):
                norm_stats(b, "c", x_res)
                normalize(b, "c", x_res, rstd12, (S["c_rstd2"], at(b, 2, 2)))
                dve.wait_ge(S["xs_s"], at(b, 1, 1))
                last_x, x = xs_t[:, 0:SEQ], xs_t[:, 1:]
                dve.tensor_tensor(delta[:], x, last_x, ALU.subtract).then_inc(S["delta_s"], 1)
                dve.wait_ge(S["delta_s"], at(b, 1, 1))
                for i, m in enumerate((mix_k, mix_v, mix_r)):
                    dve.scalar_tensor_tensor(mixed[i][:], delta[:], m[:], last_x, ALU.mult, ALU.add
                                             ).then_inc(S["mix_s"], 1)
                dve.wait_ge(S["expk_s"], at(b, 1, 1))
                dve.wait_ge(S["wkv_v_mm"], at(b, 1, 1))
                dve.tensor_tensor_scan(den[:], td_row[:], exp_k[:], 0.0, ALU.mult, ALU.add).then_inc(S["den_s"], 1)
                dve.tensor_tensor(kv[:], ps[:, BANK_B, :], exp_k[:], ALU.mult).then_inc(S["kv_s"], 1)
                dve.wait_ge(S["kv_s"], at(b, 1, 1))
                dve.tensor_tensor_scan(num[:], td_row[:], kv[:], 0.0, ALU.mult, ALU.add).then_inc(S["num_s"], 1)
                dve.wait_ge(S["den_s"], at(b, 1, 1))
                dve.tensor_scalar(den_eps[:], den[:], WKV_EPS, None, ALU.add).then_inc(S["deneps_s"], 1)
                dve.wait_ge(S["expr_s"], at(b, 1, 1))
                dve.wait_ge(S["deneps_s"], at(b, 1, 1))
                dve.scalar_tensor_tensor(den[:], exp_r[:], 1.0, den_eps[:], ALU.add, ALU.mult).then_inc(S["denr_s"], 1)
                dve.wait_ge(S["denr_s"], at(b, 1, 1))
                dve.reciprocal(wkv_inv[:], den[:]).then_inc(S["winv_s"], 1)
                dve.wait_ge(S["winv_s"], at(b, 1, 1))
                dve.wait_ge(S["num_s"], at(b, 1, 1))
                dve.tensor_tensor(wkv[:], num[:], wkv_inv[:], ALU.mult).then_inc(S["wkv_s"], 1)
                dve.wait_ge(S["wkvo_mm"], at(b, 1, 1))
                norm_stats(b, "co", bank4(BANK_B))
                normalize(b, "co", bank4(BANK_B))
                add_residual(b, "co", x_res, x_res, "res_c")

            def experts(b):
                norm_stats(b, "d", x_res)
                normalize(b, "d", x_res)
                wide = [P, NT, EXPERTS]
                dve.wait_ge(S["gate_mm"], at(b, 1, 1))
                dve.tensor_copy(gates[:], ps[:, BANK_B, 0:NT * EXPERTS].rearrange("p (t e) -> p t e", t=NT)
                                ).then_inc(S["gates_s"], 1)
                dve.wait_ge(S["loaded"], LOADED)
                dve.wait_ge(S["gates_s"], at(b, 1, 1))
                for i in range(NT):
                    last = dve.max(top[:, i, :], gates[:, i, :])
                last.then_inc(S["top_s"], 1)
                dve.wait_ge(S["top_s"], at(b, 1, 1))
                dve.tensor_tensor(gate_sh[:], gates[:], top[:, :, 0:1].to_broadcast(wide), ALU.subtract
                                  ).then_inc(S["gshift_s"], 1)
                dve.tensor_tensor(chosen[:], gates[:], top[:, :, 1:2].to_broadcast(wide), ALU.is_ge
                                  ).then_inc(S["chosen_s"], 1)
                dve.wait_ge(S["gexp_s"], at(b, 1, 1))
                dve.wait_ge(S["chosen_s"], at(b, 1, 1))
                dve.tensor_tensor(gate_kept[:], gate_exp[:], chosen[:], ALU.mult).then_inc(S["gkept_s"], 1)
                dve.wait_ge(S["gkept_s"], at(b, 1, 1))
                dve.tensor_reduce(gate_sum[:], gate_kept[:], AX.X, ALU.add).then_inc(S["gsum_s"], 1)
                dve.wait_ge(S["gsum_s"], at(b, 1, 1))
                dve.reciprocal(gate_inv[:], gate_sum[:]).then_inc(S["ginv_s"], 1)
                dve.wait_ge(S["ginv_s"], at(b, 1, 1))
                dve.scalar_tensor_tensor(share[:], gate_kept[:], 1.0 / EXPERTS,
                                         gate_inv[:].unsqueeze(2).to_broadcast(wide), ALU.mult, ALU.mult
                                         ).then_inc(S["share_s"], 1)
                dve.wait_ge(S["share_s"], at(b, 1, 1))
                part = [share_parts[:, :, k * EXPERTS:(k + 1) * EXPERTS] for k in range(3)]
                dve.tensor_copy(part[0], share[:]).then_inc(S["shi_s"], 1)
                dve.wait_ge(S["shi_s"], at(b, 1, 1))
                dve.tensor_tensor(share_rest[:], share[:], part[0], ALU.subtract).then_inc(S["srest_s"], 1)
                dve.wait_ge(S["srest_s"], at(b, 1, 1))
                dve.tensor_copy(part[1], share_rest[:]).then_inc(S["smid_s"], 1)
                dve.wait_ge(S["smid_s"], at(b, 1, 1))
                dve.tensor_tensor(part[2], share_rest[:], part[1], ALU.subtract).then_inc(S["slo_s"], 1)
                for n in range(EXPERTS * HB):
                    e = n // HB
                    dve.wait_ge(S["z_mm"], at(b, n + 1, EXPERTS * HB))
                    dve.wait_ge(S["row_s"], at(b, e + 1, EXPERTS))
                    dve.scalar_tensor_tensor(hidden[:, n % 2, :], ps[:, BANK_MAX[n % 2], :], neg_b1[:, n:n + 1],
                                             share_row[:, e % 2, :], ALU.max, ALU.mult).then_inc(S["hidden_s"], 1)
                dve.wait_ge(S["yt_mm"], at(b, 1, 1))
                norm_stats(b, "do", bank4(BANK_C))
                normalize(b, "do", bank4(BANK_C))
                dve.wait_ge(S["out_stored"], at(b, 1, 1) * 16)
                add_residual(b, "do", x_res, result, "res_d")

            with dve.Fori(0, BATCH) as b:
                dve.wait_ge(S["x_loaded"], at(b, 1, 1) * 16)
                norm_stats(b, "a", x_in)
                normalize(b, "a", x_in)
                qkv(b)
                attention(b)
                lora(b)
                time_mix(b)
                experts(b)


_OUT = (BATCH, SEQ, D)


def shape_constants():
    def bits(v):
        return (np.ascontiguousarray(v, dtype=np.float32).view(np.uint32) >> 16).astype(np.uint16)

    slopes = 0.5 ** np.arange(HEADS, dtype=np.float64)
    pos = np.arange(P)
    dist = -np.abs(pos[:, None] - pos[None, :])
    diag = bits(dist[:, None, :] * slopes[None, :, None])
    block, inner = np.arange(SEQ) // P, np.arange(SEQ) % P
    q_rows = np.zeros((CONST_ROWS, HEADS, SEQ))
    k_rows = np.zeros((CONST_ROWS, HEADS, SEQ))
    for r in range(NT):
        q_rows[r] = np.sign(block - r)
        k_rows[r] = slopes[:, None] * (inner * (block == r))
        q_rows[NT + r] = inner * (block == r)
        k_rows[NT + r] = -slopes[:, None] * np.sign(r - block)
        q_rows[2 * NT + r] = -P * np.abs(block - r)
        k_rows[2 * NT + r] = slopes[:, None] * (block == r)
    k_rows[3 * NT:] = 1.0
    pick = np.zeros((P, EXPERTS, P))
    for e in range(EXPERTS):
        for k in range(3):
            pick[k * EXPERTS + e, e, :] = 1.0
    return {"ident": np.eye(P, dtype=np.float32), "identb": bits(np.eye(P)), "diag": diag,
            "q_rows": bits(q_rows), "k_rows": bits(k_rows), "pick": bits(pick)}


def kernel(**inputs):
    import concourse.bacc as bacc
    from concourse.bass_utils import run_bass_kernel_spmd as run

    a = {k: np.asarray(v) for k, v in inputs.items()}
    c = np.ascontiguousarray
    w_heads = a["L0_attn_qkv_w"].reshape(HEADS, 3, DH, D)
    b_heads = a["L0_attn_qkv_b"].reshape(HEADS, 3, DH)
    col = lambda v: c(v.reshape(D, 1))
    arrays = {
        "x": a["L0_attn_x"],
        "wq": c(w_heads[:, 0].reshape(D, D).T), "wk": c(w_heads[:, 1].reshape(D, D).T),
        "wv": c(w_heads[:, 2].reshape(D, D).T), "wo": c(a["L0_attn_out_w"].T),
        "bq": col(b_heads[:, 0]), "bk": col(b_heads[:, 1]), "bv": c(b_heads[:, 2].reshape(D)),
        "bo": a["L0_attn_out_b"],
        "route_w": c(a["L0_ffn_router_w"].T), "route_b": a["L0_ffn_router_b"], "lora_a": a["L0_ffn_lora_A"],
        "lora_b": c(a["L0_ffn_lora_B"].reshape(LORA_E * RANK, D)), "base_w": c(a["L0_ffn_base_w"].T),
        "base_b": a["L0_ffn_base_b"].reshape(1, D),
        "decay": col(a["L1_attn_time_decay"]), "ln_g": col(a["L1_attn_ln_g"]), "ln_b": col(a["L1_attn_ln_b"]),
        "mix_k": col(a["L1_attn_time_mix_k"]), "mix_v": col(a["L1_attn_time_mix_v"]),
        "mix_r": col(a["L1_attn_time_mix_r"]),
        "wkk": c(a["L1_attn_Wk"].T), "wkv": c(a["L1_attn_Wv"].T), "wkr": c(a["L1_attn_Wr"].T),
        "wko": c(a["L1_attn_Wo"].T),
        "w_gate": a["L1_ffn_W_gate"], "w1": a["L1_ffn_W1"], "w2": a["L1_ffn_W2"],
        "b1": c(a["L1_ffn_b1"].reshape(EXPERTS * HB, P).T), "b2": a["L1_ffn_b2"],
    }
    arrays.update(shape_constants())
    nc = bacc.Bacc("TRN2", target_bir_lowering=False, num_devices=1)
    t = {k: nc.dram_tensor(f"in_{k}", v.shape, mybir.dt.from_np(v.dtype), kind="ExternalInput").ap()
         for k, v in arrays.items()}
    t.update({k: t[k].bitcast(BF16) for k in ("identb", "diag", "q_rows", "k_rows", "pick")})
    t["out"] = nc.dram_tensor("out", _OUT, F32, kind="ExternalOutput").ap()
    t["parts"] = nc.dram_tensor("qk_parts_dram", (2, 3, P, SEQ), BF16, kind="Internal").ap()
    layer_norms_attention_lora_wkv_moe_kernel(nc, t)
    r = run(nc, [{f"in_{k}": v for k, v in arrays.items()}], core_ids=[0])
    return r.results[0]["out"]
```

```python
from contextlib import ExitStack

import numpy as np

import concourse.bass as bass
from concourse import mybir

F32 = mybir.dt.float32
BF16 = mybir.dt.bfloat16
ALU = mybir.AluOpType
ACT = mybir.ActivationFunctionType
AX = mybir.AxisListType

P = 128
BATCH, SEQ, D = 8, 512, 128
NT = SEQ // P
HEADS, DH = 16, 8
HG = 4
GROUPS = HEADS // HG
EXPERTS, HID = 8, 512
HB = HID // P
RANK, LORA_E = 8, 8
LORA_SCALE = 16.0 / RANK
EPS = 1e-5
WKV_EPS = 1e-8

SLOTS = [(0, 0), (0, 1), (1, 0), (1, 1), (0, 2), (2, 0)]
BIAS_ROW = DH * len(SLOTS)
MAX_ROW = BIAS_ROW + 3 * NT
CONST_ROWS = 3 * NT + 2

UNITS = HEADS * NT
LEAD = 8
STEPS = GROUPS * NT

BANK_MAX = (0, 1)
BANK_EXP = (2, 3)
BANK_OUT = 4
BANK_A, BANK_B, BANK_C = 5, 6, 7

EARLY_STEPS = 2
FILL = """lora_t lora_route lora_logits lora_exp lora_outer lora_outer_t lora_mm lora_stats lora_res
    - - wkv_norm wkv_t wkv_mix1 wkv_k wkv_v wkv_scan wkv_gate wkv_out wkv_stats wkv_res
    - moe_norm moe_t moe_gate moe_top moe_exp moe_share""".split()
FINISH = ["moe_sum_t", "moe_sum_stats", "moe_res"]
UNITS_E = EXPERTS * HB
BESIDE = {0: (("qk_mm", "n"), ("head_norm3", "i")), 1: (("qk_scale", "n"), ("v_mm", "n")),
          2: (("qk_hi", "n"), ("v_bias", "n"), ("heads_t", "i")), 3: (("attn_mm", "i"),),
          4: (("qk_mid", "n"), ("attn_stats", "i")), 6: (("attn_res", "i"), ("stacks", "n")),
          8: (("lora_norm", "i"),)}
ROWS_AT = {0: (0,), **{HB * e - 3: (e,) for e in range(1, EXPERTS)}}
FIRST_MAX = 13


def timeline(q, i, n):
    seq = {"q": q, "i": i, "n": n}
    yield "loads", i, n
    slots = [(f, q, None) for f in FILL]
    slots[25] = [slots[25], ("pre_stats", n, None)]
    slots[27] = [slots[27], ("pre_norm", n, None)]
    slots = iter(slots)
    for s in range(EARLY_STEPS, STEPS):
        for h4 in range(HG):
            yield "score", i, (s, h4)
            if h4 % 2:
                f = next(slots)
                yield from f if isinstance(f, list) else [f]
        yield from step_end(i, s)
    yield "weigh", i, STEPS - 1
    yield "head_out", i, GROUPS - 1
    yield "pre_t", n, None
    yield "share_t", q, None
    yield "head_t", i, GROUPS - 1
    u = 0
    for k in range(UNITS_E):
        yield "expert", q, k
        for name, who in BESIDE.get(k, ()):
            yield name, seq[who], None
        if k >= FIRST_MAX:
            left = HG * NT + LEAD - u
            for _ in range(min(left, 2 if left > UNITS_E - k else 1)):
                yield "score_max", n, u
                u += 1
                if u == HG * NT + LEAD // 2:
                    yield "max_t", n, 0
    yield "expert_sum", q, None
    finish = iter([(f, q, None) for f in FINISH])
    for s in range(EARLY_STEPS):
        for h4 in range(HG):
            yield "score", n, (s, h4)
            if h4 % 2 and (f := next(finish, None)):
                yield f
        yield from step_end(n, s)


def step_end(i, s):
    if s > 0:
        yield "weigh", i, s - 1
    if s % NT == 0 and s > 0:
        yield "head_out", i, s // NT - 1
    if s % NT == 1 and s > NT:
        yield "head_t", i, s // NT - 1
    if s % NT == 2:
        if s > NT:
            yield "head_norm", i, s // NT - 1
        if s // NT + 1 < GROUPS:
            yield "max_t", i, s // NT + 1


def opening():
    for name in ("first_load", "pre_stats", "pre_norm", "pre_t", "qk_mm", "qk_scale", "v_mm", "qk_hi", "v_bias", "qk_mid",
                 "stacks"):
        yield name, 0, None
    for u in range(HG * NT + LEAD):
        yield "score_max", 0, u
        if u + 1 == HG * NT + LEAD // 2:
            yield "max_t", 0, 0
    for s in range(EARLY_STEPS):
        for h4 in range(HG):
            yield "score", 0, (s, h4)
        yield from step_end(0, s)


def run_pieces(order, pieces):
    for name, seq, arg in order:
        if seq is not None and name in pieces:
            pieces[name](seq, arg) if arg is not None else pieces[name](seq)


def rounds(eng, pieces):
    run_pieces(opening(), pieces)
    run_pieces(timeline(None, 0, 1), pieces)
    with eng.Fori(0, BATCH - 2) as q:
        run_pieces(timeline(q, q + 1, q + 2), pieces)
    run_pieces(timeline(BATCH - 2, BATCH - 1, None), pieces)
    run_pieces(timeline(BATCH - 1, None, None), pieces)


def at(b, k, of):
    return b * of + k


def layer_norms_attention_lora_wkv_moe_kernel(nc, t):
    ctx = ExitStack()
    with ctx:
        def sb(name, shape, dt=F32):
            return ctx.enter_context(nc.sbuf_tensor(name, shape, dt))

        def sem(name):
            return ctx.enter_context(nc.semaphore(name))

        ps = ctx.enter_context(nc.psum_tensor("ps", [P, 8, SEQ], F32))

        def bank4(n, w=D):
            return ps[:, n, 0:NT * w].rearrange("p (t w) -> p t w", t=NT)

        ident = sb("ident", [P, P])
        identb = sb("identb", [P, P], BF16)
        diag = sb("diag", [P, HEADS, P], BF16)
        wq, wk, wv, wo = (sb(n, [P, D]) for n in ("wq", "wk", "wv", "wo"))
        bq, bk = sb("bq", [P, 1]), sb("bk", [P, 1])
        bv, bo = sb("bv", [P, D]), sb("bo", [P, D])
        w_rm = sb("w_rm", [P, LORA_E + RANK])
        b_route = sb("b_route", [P, LORA_E])
        w_base = sb("w_base", [P, D])
        lora_b = sb("lora_b", [P, D])
        decay, ln_g, ln_b = sb("decay", [P, 1]), sb("ln_g", [P, 1]), sb("ln_b", [P, 1])
        mix_k, mix_v, mix_r = sb("mix_k", [P, 1]), sb("mix_v", [P, 1]), sb("mix_r", [P, 1])
        wkk, wkv_, wkr, wko = (sb(n, [P, D]) for n in ("wkk", "wkv_", "wkr", "wko"))
        w_gate = sb("w_gate", [P, EXPERTS])
        w1 = sb("w1", [P, EXPERTS, HID])
        w2 = sb("w2", [P, EXPERTS * HB, D])
        b1 = sb("b1", [P, EXPERTS * HB])
        neg_b1 = sb("neg_b1", [P, EXPERTS * HB])
        b2x3 = sb("b2x3", [3 * EXPERTS, D])
        pick = sb("pick", [P, EXPERTS, P], BF16)
        skip = sb("skip", [3 * EXPERTS, D])
        skip_rest = sb("skip_rest", [3 * EXPERTS, 2, D])
        skip_parts = sb("skip_parts", [P, 3, D], BF16)
        ones = sb("ones", [P, SEQ])
        td = sb("td", [P, 1])
        free_marks = sb("free_marks", [P, 4])
        td_row = sb("td_row", [P, SEQ])
        minus_half = sb("minus_half", [P, NT])
        eps = sb("eps", [P, NT])

        x_in = sb("x_in", [P, NT, D])
        x_skip = sb("x_skip", [P, NT, D])
        x_attn = sb("x_attn", [P, NT, D])
        x_res = sb("x_res", [P, NT, D])
        LN = ("a", "ao", "b", "bo", "c", "co", "d", "do")
        stats = {n: sb(f"stats_{n}", [P, NT, 6]) for n in LN}
        moments = {n: sb(f"moments_{n}", [P, NT, 2]) for n in LN}
        var_eps = {n: sb(f"var_eps_{n}", [P, NT]) for n in LN}
        rstd = {n: sb(f"rstd_{n}", [P, NT]) for n in LN}
        normed = {n: sb(f"normed_{n}", [P, NT, D]) for n in LN}
        h_t = {n: sb(f"h_t_{n}", [P, SEQ]) for n in ("a", "b", "d")}
        qk = [sb(f"qk{i}", [P, SEQ]) for i in range(2)]
        qk_rest = [sb(f"qk_rest{i}", [P, SEQ]) for i in range(2)]
        qk_parts = [sb(f"qk_parts{i}", [P, 3, SEQ], BF16) for i in range(2)]
        q_stack = sb("q_stack", [P, HEADS, SEQ], BF16)
        k_stack = sb("k_stack", [P, HEADS, SEQ], BF16)
        v_aug = sb("v_aug", [P, NT, HEADS, 32])
        maxima = sb("maxima", [P, 2, HG * NT])
        max_hi = sb("max_hi", [HG * NT, 2, P], BF16)
        max_lo = sb("max_lo", [HG * NT, 2, P], BF16)
        probs = sb("probs", [P, 2, HG, SEQ])
        b1_col = probs[:, 0, :, :].rearrange("p h n -> p (h n)")[:, 0:EXPERTS * HB * 3 * EXPERTS].rearrange(
            "p (n c) -> p n c", c=3 * EXPERTS)
        heads_t = sb("heads_t", [P, SEQ])
        inv_sum = sb("inv_sum", [P, NT, HG])
        heads = sb("heads", [P, NT, HEADS, DH])
        heads_all_t = sb("heads_all_t", [P, SEQ])
        attn = sb("attn", [P, NT, D])
        logits = sb("logits", [P, NT, LORA_E])
        route_max = sb("route_max", [P, NT])
        shifted = sb("shifted", [P, NT, LORA_E])
        route_exp = sb("route_exp", [P, NT, LORA_E])
        route_sum = sb("route_sum", [P, NT])
        route_inv = sb("route_inv", [P, NT])
        gating = sb("gating", [P, NT, LORA_E], BF16)
        mid = sb("mid", [P, NT, RANK])
        outer = sb("outer", [P, NT, P])
        outer_t = sb("outer_t", [P, SEQ])
        var1 = sb("var1", [P, NT])
        rstd2 = sb("rstd2", [P, NT])
        rstd12 = sb("rstd12", [P, NT])
        xs_t = sb("xs_t", [P, 1 + SEQ])
        delta = sb("delta", [P, SEQ])
        mixed = [sb(f"mixed{i}", [P, SEQ]) for i in range(3)]
        exp_k = sb("exp_k", [P, SEQ])
        exp_r = sb("exp_r", [P, SEQ])
        kv = sb("kv", [P, SEQ])
        den = sb("den", [P, SEQ])
        num = sb("num", [P, SEQ])
        den_eps = sb("den_eps", [P, SEQ])
        wkv = sb("wkv", [P, SEQ])
        gates = sb("gates", [P, NT, EXPERTS])
        top = sb("top", [P, NT, 8])
        chosen = sb("chosen", [P, NT, EXPERTS])
        gate_sh = sb("gate_sh", [P, NT, EXPERTS])
        gate_exp = sb("gate_exp", [P, NT, EXPERTS])
        gate_kept = sb("gate_kept", [P, NT, EXPERTS])
        gate_sum = sb("gate_sum", [P, NT])
        gate_inv = sb("gate_inv", [P, NT])
        share = sb("share", [P, NT, EXPERTS])
        share_rest = sb("share_rest", [P, NT, EXPERTS])
        share_parts = sb("share_parts", [P, NT, P], BF16)
        share_t = sb("share_t", [P, SEQ], BF16)
        share_row = sb("share_row", [P, 2, SEQ])
        hidden = sb("hidden", [P, 2, SEQ])
        moe_t = sb("moe_t", [P, SEQ])
        result = sb("result", [P, NT, D])

        names = [f"{a}_{n}" for n in LN for a in ("stats", "moments", "vareps", "rstd", "normed")]
        names += """loaded cleared consts_ready skip_mm x_skip_loaded skip_sum skip_hi skip_rest skip_done td_done
            x_loaded out_stored res_a res_b res_c res_d
            ht_a_mm ht_a qk_mm v_mm qk_scaled qk_hi qk_rest1 qk_mid qk_lo v_done parts_stored
            stacks_loaded s1_ready s1_used max_mm max_hi_s max_lo_s mrow0 mrow1
            s2_ready probs_done pv_done ov_done heads_t_s heads_mm inv_s heads_s heads_all_mm heads_all_s
            attn_mm attn_s
            ht_b_mm ht_b rm_mm logits_s rmax_s rshift_s rexp_s rsum_s rinv_s gating_s mid_s outer_s
            outer_mm outer_t_s lora_mm
            c_var1 c_vareps2 c_rstd2 xs_mm xs_s delta_s mix_s wkv_k_mm wkv_v_mm wkv_r_mm expk_s expr_s kv_s
            den_s num_s deneps_s denr_s winv_s wkv_s wkvo_mm
            ht_d_mm ht_d gate_mm gates_s top_s chosen_s gshift_s gexp_s gkept_s gsum_s ginv_s share_s
            shi_s srest_s smid_s slo_s share_mm share_t_s row_mm row_s z_mm hidden_s y_mm y_s yt_mm
            """.split()
        S = {n: sem(n) for n in names}

        block = ctx.enter_context(nc.Block())

        loads = [
            (ident[:], t["ident"]), (identb[:], t["identb"]), (diag[:], t["diag"]),
            (wq[:], t["wq"]), (wk[:], t["wk"]), (wv[:], t["wv"]), (wo[:], t["wo"]),
            (bq[:], t["bq"]), (bk[:], t["bk"]),
            (bv[:], t["bv"].partition_broadcast(P)), (bo[:], t["bo"].partition_broadcast(P)),
            (w_rm[:, 0:LORA_E], t["route_w"]), (w_rm[:, LORA_E:], t["lora_a"]),
            (b_route[:], t["route_b"].partition_broadcast(P)), (w_base[:], t["base_w"]),
            (decay[:], t["decay"]), (ln_g[:], t["ln_g"]), (ln_b[:], t["ln_b"]),
            (mix_k[:], t["mix_k"]), (mix_v[:], t["mix_v"]), (mix_r[:], t["mix_r"]),
            (wkk[:], t["wkk"]), (wkv_[:], t["wkv"]), (wkr[:], t["wkr"]), (wko[:], t["wko"]),
            (w_gate[:], t["w_gate"]), (b1[:], t["b1"]),
            (b2x3[0:8, :], t["b2"]), (b2x3[8:16, :], t["b2"]), (b2x3[16:24, :], t["b2"]),
            (pick[:], t["pick"]),
            (w1[:], t["w1"].rearrange("e d h -> d e h")),
            (w2[:], t["w2"].rearrange("e (n p) d -> p (e n) d", p=P)),
        ]
        late_loads = [
            (q_stack[BIAS_ROW:BIAS_ROW + CONST_ROWS, :, :], t["q_rows"]),
            (k_stack[BIAS_ROW:BIAS_ROW + CONST_ROWS, :, :], t["k_rows"]),
            (lora_b[0:LORA_E * RANK, :], t["lora_b"]), (lora_b[LORA_E * RANK:LORA_E * RANK + 1, :], t["base_b"]),
        ]
        LOADED = 16 * (len(loads) + len(late_loads))
        SLOT_DMAS = 2 * len(SLOTS) + 1
        CLEARS = 2

        def unit(u):
            return u // (HG * NT), u // NT % HG + u // (HG * NT) * HG, u % NT

        @block.sync
        def _(sp):
            for dst, src in loads:
                sp.dma_start(dst, src).then_inc(S["loaded"], 16)
            sp.wait_ge(S["cleared"], CLEARS)
            for dst, src in late_loads:
                sp.dma_start(dst, src).then_inc(S["loaded"], 16)

            def fetch(dst, b, done):
                sp.dma_start(dst[:], t["x"][bass.ds(b, 1), :, :].rearrange("o (t p) d -> p (o t) d", p=P)
                             ).then_inc(S[done], 16)

            def loads_x(i, n=None):
                if i is not None:
                    if not isinstance(i, int) or i > 0:
                        sp.wait_ge(S["res_a"], at(i, 0, 1))
                    fetch(x_skip, i, "x_skip_loaded")
                if n is not None:
                    sp.wait_ge(S["normed_a"], at(n, 0, 1))
                    fetch(x_in, n, "x_loaded")

            def build_stacks(b):
                for i, n in ((0, 1), (1, 2)):
                    sp.wait_ge(S["qk_lo"], at(b, n, 2))
                    sp.wait_ge(S["qk_mid"], at(b, n, 2))
                    sp.dma_start(t["parts"][i].rearrange("k p n -> p k n"), qk_parts[i][:]
                                 ).then_inc(S["parts_stored"], 16)
                sp.wait_ge(S["parts_stored"], at(b, 1, 1) * 32)
                for s, pair in enumerate(SLOTS):
                    for i, stack in ((0, q_stack), (1, k_stack)):
                        sp.dma_start(stack[DH * s:DH * s + DH, :, :],
                                     t["parts"][i, pair[i]].rearrange("(h d) n -> d h n", d=DH)
                                     ).then_inc(S["stacks_loaded"], 16)
                sp.dma_start(q_stack[MAX_ROW:MAX_ROW + 2, :, :], t["q_rows"][3 * NT:3 * NT + 2]
                             ).then_inc(S["stacks_loaded"], 16)

            def max_rows(b, g):
                dst = q_stack[:, HG * g:HG * g + HG, :]
                sp.wait_ge(S["max_lo_s"], at(b, g + 1, GROUPS))
                for k, src in ((0, max_hi), (1, max_lo)):
                    sp.dma_start(dst[MAX_ROW + k:MAX_ROW + k + 1].rearrange("p h (i c) -> p (h i) c", c=P),
                                 src[:, g % 2, :]).then_inc(S[f"mrow{g % 2}"], 16)

            def store(b):
                sp.wait_ge(S["res_d"], at(b, 1, 1))
                sp.dma_start(t["out"][bass.ds(b, 1), :, :].rearrange("o (t p) d -> p (o t) d", p=P), result[:]
                             ).then_inc(S["out_stored"], 16)

            rounds(sp, {"first_load": lambda b: fetch(x_in, b, "x_loaded"), "loads": loads_x,
                        "stacks": build_stacks, "max_t": max_rows, "moe_res": store})
            sp.wait_ge(S["out_stored"], 16 * (BATCH + 1))

        @block.gpsimd
        def _(pool):
            pool.memset(q_stack[:], 0.0)
            pool.memset(k_stack[:], 0.0)
            pool.memset(lora_b[:], 0.0).then_inc(S["cleared"], 1)
            pool.memset(v_aug[:], 0.0)
            pool.memset(share_parts[:], 0.0)
            pool.memset(outer[:], 0.0)
            pool.memset(skip_parts[:], 0.0)
            pool.memset(b1_col, 0.0)
            pool.memset(minus_half[:], -0.5)
            pool.memset(eps[:], EPS)
            pool.memset(xs_t[:, 0:1], 0.0).then_inc(S["cleared"], 1)
            pool.wait_ge(S["cleared"], 2)

            def rsqrt(b, n):
                pool.wait_ge(S[f"moments_{n}"], at(b, 1, 1))
                pool.tensor_tensor(var_eps[n][:], moments[n][:, :, 1], eps[:], ALU.add
                                   ).then_inc(S[f"vareps_{n}"], 1)
                pool.wait_ge(S[f"vareps_{n}"], at(b, 1, 1))
                pool.tensor_tensor(rstd[n][:], var_eps[n][:], minus_half[:], ALU.pow
                                   ).then_inc(S[f"rstd_{n}"], 1)

            def rsqrt_twice(b):
                pool.wait_ge(S["rstd_c"], at(b, 1, 1))
                pool.tensor_tensor(var1[:], moments["c"][:, :, 1], rstd["c"][:], ALU.mult).then_inc(S["c_var1"], 1)
                pool.wait_ge(S["c_var1"], at(b, 1, 2))
                pool.tensor_tensor(var1[:], var1[:], rstd["c"][:], ALU.mult).then_inc(S["c_var1"], 1)
                pool.wait_ge(S["c_var1"], at(b, 2, 2))
                pool.tensor_tensor(var1[:], var1[:], eps[:], ALU.add).then_inc(S["c_vareps2"], 1)
                pool.wait_ge(S["c_vareps2"], at(b, 1, 1))
                pool.tensor_tensor(rstd2[:], var1[:], minus_half[:], ALU.pow).then_inc(S["c_rstd2"], 1)
                pool.wait_ge(S["c_rstd2"], at(b, 1, 2))
                pool.tensor_tensor(rstd12[:], rstd2[:], rstd["c"][:], ALU.mult).then_inc(S["c_rstd2"], 1)

            def split_rest(b):
                for i in range(2):
                    pool.wait_ge(S["qk_hi"], at(b, i + 1, 2))
                    pool.tensor_tensor(qk_rest[i][:], qk[i][:], qk_parts[i][:, 0, :], ALU.subtract
                                       ).then_inc(S["qk_rest1"], 1)

            def split_low(b):
                for i in range(2):
                    pool.wait_ge(S["qk_mid"], at(b, i + 1, 2))
                    pool.tensor_tensor(qk_parts[i][:, 2, :], qk_rest[i][:], qk_parts[i][:, 1, :], ALU.subtract
                                       ).then_inc(S["qk_lo"], 1)

            def lora_res(b):
                rsqrt(b, "c")
                rsqrt_twice(b)

            rounds(pool, {
                "pre_stats": lambda b: rsqrt(b, "a"), "qk_hi": split_rest, "qk_mid": split_low,
                "attn_stats": lambda b: rsqrt(b, "ao"), "attn_res": lambda b: rsqrt(b, "b"),
                "lora_stats": lambda b: rsqrt(b, "bo"), "lora_res": lora_res,
                "wkv_stats": lambda b: rsqrt(b, "co"), "wkv_res": lambda b: rsqrt(b, "d"),
                "moe_sum_stats": lambda b: rsqrt(b, "do")})

        @block.scalar
        def _(act):
            act.wait_ge(S["loaded"], LOADED)
            act.activation(td[:], decay[:], ACT.Exp).then_inc(S["td_done"], 1)

            def transposed(b, n):
                act.wait_ge(S[f"ht_{n}_mm"], at(b, 1, 1))
                act.activation(h_t[n][:], ps[:, {"a": BANK_MAX[0], "b": BANK_B, "d": BANK_C}[n], :], ACT.Copy
                               ).then_inc(S[f"ht_{n}"], 1)

            def high(b):
                for i in range(2):
                    act.wait_ge(S["qk_scaled"], at(b, i + 1, 2))
                    act.activation(qk_parts[i][:, 0, :], qk[i][:], ACT.Copy).then_inc(S["qk_hi"], 1)

            def middle(b):
                for i in range(2):
                    act.wait_ge(S["qk_rest1"], at(b, i + 1, 2))
                    act.activation(qk_parts[i][:, 1, :], qk_rest[i][:], ACT.Copy).then_inc(S["qk_mid"], 1)

            def exps(b, where):
                s, h = where
                if s >= 2 and h == 0:
                    act.wait_ge(S["pv_done"], at(b, s - 1, STEPS))
                n = HG * s + h
                act.wait_ge(S["s2_ready"], at(b, n + 1, UNITS))
                act.activation(probs[:, s % 2, h, :], ps[:, BANK_EXP[n % 2], :], ACT.Exp
                               ).then_inc(S["probs_done"], 1)

            def head_out(b, g):
                act.wait_ge(S["pv_done"], at(b, NT * (g + 1), STEPS))
                act.activation(heads_t[:], ps[:, BANK_OUT, :], ACT.Copy).then_inc(S["heads_t_s"], 1)

            def heads_transposed(b):
                act.wait_ge(S["heads_all_mm"], at(b, 1, 1))
                act.activation(heads_all_t[:], ps[:, BANK_A, :], ACT.Copy).then_inc(S["heads_all_s"], 1)

            def route_exps(b):
                act.wait_ge(S["rshift_s"], at(b, 1, 1))
                act.activation(route_exp[:], shifted[:], ACT.Exp).then_inc(S["rexp_s"], 1)

            def outer_transposed(b):
                act.wait_ge(S["outer_mm"], at(b, 1, 1))
                act.activation(outer_t[:], ps[:, BANK_C, :], ACT.Copy).then_inc(S["outer_t_s"], 1)

            def wkv_transposed(b):
                act.wait_ge(S["xs_mm"], at(b, 1, 1))
                act.activation(xs_t[:, 1:], ps[:, BANK_B, :], ACT.Identity, bias=ln_b[:], scale=ln_g[:]
                               ).then_inc(S["xs_s"], 1)

            def exp_keys(b):
                act.wait_ge(S["wkv_k_mm"], at(b, 1, 1))
                act.activation(exp_k[:], ps[:, BANK_C, :], ACT.Exp).then_inc(S["expk_s"], 1)

            def exp_receptance(b):
                act.wait_ge(S["wkv_r_mm"], at(b, 1, 1))
                act.activation(exp_r[:], ps[:, BANK_C, :], ACT.Exp, scale=-1.0).then_inc(S["expr_s"], 1)

            def gate_exps(b):
                act.wait_ge(S["gshift_s"], at(b, 1, 1))
                act.activation(gate_exp[:], gate_sh[:], ACT.Exp).then_inc(S["gexp_s"], 1)

            def shares_transposed(b):
                act.wait_ge(S["share_mm"], at(b, 1, 1))
                act.activation(share_t[:], ps[:, BANK_B, :].bitcast(BF16)[:, 0:SEQ], ACT.Copy
                               ).then_inc(S["share_t_s"], 1)

            def share_rows(b, k):
                for e in ROWS_AT.get(k, ()):
                    act.wait_ge(S["row_mm"], at(b, e + 1, EXPERTS))
                    if e >= 2:
                        act.wait_ge(S["hidden_s"], at(b, HB * (e - 1), UNITS_E))
                    act.activation(share_row[:, e % 2, :], ps[:, BANK_C, :], ACT.Copy).then_inc(S["row_s"], 1)

            def expert_sum(b):
                act.wait_ge(S["y_mm"], at(b, 1, 1))
                act.activation(moe_t[:], ps[:, BANK_OUT, :], ACT.Copy).then_inc(S["y_s"], 1)

            rounds(act, {
                "pre_t": lambda b: transposed(b, "a"), "qk_hi": high, "qk_mid": middle, "score": exps,
                "head_out": head_out, "heads_t": heads_transposed,
                "lora_t": lambda b: transposed(b, "b"), "lora_exp": route_exps, "lora_outer_t": outer_transposed,
                "wkv_t": wkv_transposed, "wkv_k": exp_keys, "wkv_v": exp_receptance,
                "moe_t": lambda b: transposed(b, "d"), "moe_exp": gate_exps, "share_t": shares_transposed,
                "expert": share_rows, "expert_sum": expert_sum})

        @block.tensor
        def _(pe):
            pe.wait_ge(S["loaded"], LOADED)
            pe.wait_ge(S["cleared"], 2)

            def mm(out, lhs, rhs, start=True, stop=True, **kw):
                return pe.matmul(out, lhs, rhs, start=start, stop=stop, skip_group_check=True, **kw)

            pe.wait_ge(S["consts_ready"], 1)
            for n in range(EXPERTS * HB):
                last = mm(ps[0:3 * EXPERTS, BANK_A, 0:D], b1_col[:, n, :], w2[:, n, :],
                          start=(n == 0), stop=(n == EXPERTS * HB - 1))
            last.then_inc(S["skip_mm"], 1)

            def transposes(b, n, bank, done):
                pe.wait_ge(S[f"normed_{n}"], at(b, 1, 1))
                for i in range(NT):
                    last = pe.transpose(ps[:, bank, i * P:(i + 1) * P], normed[n][:, i, :], ident[:])
                last.then_inc(S[done], 1)

            def project(b):
                pe.wait_ge(S["ht_a"], at(b, 1, 1))
                mm(ps[:, BANK_B, :], wq[:], h_t["a"][:]).then_inc(S["qk_mm"], 1)
                mm(ps[:, BANK_MAX[1], :], wk[:], h_t["a"][:]).then_inc(S["qk_mm"], 1)

            def project_values(b):
                for i in range(NT):
                    last = mm(ps[:, BANK_MAX[0], i * D:(i + 1) * D], h_t["a"][:, i * P:(i + 1) * P], wv[:])
                last.then_inc(S["v_mm"], 1)

            def score_max(b, u):
                _, h, i = unit(u)
                bank = ps[:, BANK_MAX[u % 2], :]
                if u == 0:
                    pe.wait_ge(S["stacks_loaded"], at(b, 1, 1) * 16 * SLOT_DMAS)
                    pe.wait_ge(S["v_done"], at(b, 1, 1))
                pe.wait_ge(S["s1_used"], at(b, u + 1, UNITS))
                mm(bank, q_stack[:, h, i * P:(i + 1) * P], k_stack[:, h, :], stop=False)
                mm(bank[:, i * P:(i + 1) * P], identb[:], diag[:, h, :], start=False
                   ).then_inc(S["s1_ready"], 1)

            def max_transpose(b, g):
                pe.wait_ge(S["s1_used"], at(b, 2 + (g + 1) * HG * NT, UNITS))
                if g >= 2:
                    pe.wait_ge(S["heads_s"], at(b, g - 1, GROUPS))
                pe.transpose(ps[0:HG * NT, BANK_A, 0:P], maxima[:, g % 2, :], ident[:]).then_inc(S["max_mm"], 1)

            def score(b, where):
                s, h4 = where
                u = HG * NT + LEAD + HG * s + h4
                if u < UNITS:
                    score_max(b, u)
                g, j = s // NT, s % NT
                h, n = HG * g + h4, HG * s + h4
                if j == 0 and h4 == 0:
                    pe.wait_ge(S[f"mrow{g % 2}"], at(b, g // 2 + 1, GROUPS // 2) * 32)
                pe.wait_ge(S["probs_done"], at(b, n + 1, UNITS))
                bank = ps[:, BANK_EXP[n % 2], :]
                mm(bank, k_stack[:, h, j * P:(j + 1) * P], q_stack[:, h, :], stop=False)
                mm(bank[:, j * P:(j + 1) * P], identb[:], diag[:, h, :], start=False
                   ).then_inc(S["s2_ready"], 1)

            def weigh_values(b, s):
                g, j = s // NT, s % NT
                pe.wait_ge(S["probs_done"], at(b, 2 + HG * (s + 1), UNITS))
                if j == 0 and g > 0:
                    pe.wait_ge(S["heads_t_s"], at(b, g, GROUPS))
                for r in range(HG):
                    last = mm(ps[32 * r:32 * r + 32, BANK_OUT, :], v_aug[:, j, HG * g + r, :],
                              probs[:, s % 2, r, :], start=(j == 0), stop=(j == NT - 1), tile_position=(0, 32 * r))
                last.then_inc(S["pv_done"], 1)

            def head_transpose(b, g):
                pe.wait_ge(S["heads_t_s"], at(b, g + 1, GROUPS))
                if g > 0:
                    pe.wait_ge(S["heads_s"], at(b, g, GROUPS))
                if g < GROUPS - 1:
                    pe.wait_ge(S["max_lo_s"], at(b, g + 2, GROUPS))
                for i in range(NT):
                    last = pe.transpose(ps[:, BANK_A, i * P:(i + 1) * P], heads_t[:, i * P:(i + 1) * P], ident[:])
                last.then_inc(S["heads_mm"], 1)

            def heads_all(b):
                pe.wait_ge(S["heads_s"], at(b, GROUPS, GROUPS))
                for i in range(NT):
                    last = pe.transpose(ps[:, BANK_A, i * P:(i + 1) * P],
                                        heads[:, i, :, :].rearrange("p h d -> p (h d)"), ident[:])
                last.then_inc(S["heads_all_mm"], 1)

            def project_out(b):
                pe.wait_ge(S["heads_all_s"], at(b, 1, 1))
                for i in range(NT):
                    last = mm(ps[:, BANK_A, i * D:(i + 1) * D], heads_all_t[:, i * P:(i + 1) * P], wo[:])
                last.then_inc(S["attn_mm"], 1)

            def route(b):
                pe.wait_ge(S["ht_b"], at(b, 1, 1))
                for i in range(NT):
                    last = mm(ps[:, BANK_C, i * 16:(i + 1) * 16], h_t["b"][:, i * P:(i + 1) * P], w_rm[:])
                last.then_inc(S["rm_mm"], 1)

            def outer_transpose(b):
                pe.wait_ge(S["outer_s"], at(b, 1, 1))
                for i in range(NT):
                    last = pe.transpose(ps[:, BANK_C, i * P:(i + 1) * P], outer[:, i, :], ident[:])
                last.then_inc(S["outer_mm"], 1)

            def lora_out(b):
                pe.wait_ge(S["outer_t_s"], at(b, 1, 1))
                for i in range(NT):
                    out = ps[:, BANK_B, i * D:(i + 1) * D]
                    mm(out, h_t["b"][:, i * P:(i + 1) * P], w_base[:], stop=False)
                    last = mm(out, outer_t[:, i * P:(i + 1) * P], lora_b[:], start=False)
                last.then_inc(S["lora_mm"], 1)

            def wkv_keys(b):
                pe.wait_ge(S["mix_s"], at(b, 1, 3))
                mm(ps[:, BANK_C, :], wkk[:], mixed[0][:]).then_inc(S["wkv_k_mm"], 1)

            def wkv_values(b):
                pe.wait_ge(S["mix_s"], at(b, 2, 3))
                mm(ps[:, BANK_B, :], wkv_[:], mixed[1][:]).then_inc(S["wkv_v_mm"], 1)
                pe.wait_ge(S["mix_s"], at(b, 3, 3))
                pe.wait_ge(S["expk_s"], at(b, 1, 1))
                mm(ps[:, BANK_C, :], wkr[:], mixed[2][:]).then_inc(S["wkv_r_mm"], 1)

            def wkv_out(b):
                pe.wait_ge(S["wkv_s"], at(b, 1, 1))
                for i in range(NT):
                    last = mm(ps[:, BANK_B, i * D:(i + 1) * D], wkv[:, i * P:(i + 1) * P], wko[:])
                last.then_inc(S["wkvo_mm"], 1)

            def gate(b):
                pe.wait_ge(S["ht_d"], at(b, 1, 1))
                for i in range(NT):
                    last = mm(ps[:, BANK_B, i * EXPERTS:(i + 1) * EXPERTS], h_t["d"][:, i * P:(i + 1) * P], w_gate[:])
                last.then_inc(S["gate_mm"], 1)

            def share_transpose(b):
                pe.wait_ge(S["slo_s"], at(b, 1, 1))
                pe.wait_ge(S["smid_s"], at(b, 1, 1))
                shares = ps[:, BANK_B, :].bitcast(BF16)
                for i in range(NT):
                    last = pe.transpose(shares[:, i * P:(i + 1) * P], share_parts[:, i, :], identb[:])
                last.then_inc(S["share_mm"], 1)

            def down(b, n):
                pe.wait_ge(S["hidden_s"], at(b, n + 1, UNITS_E))
                return mm(ps[:, BANK_OUT, :], w2[:, n, :], hidden[:, n % 2, :], start=False, stop=(n == UNITS_E - 1))

            def expert_block(b, n):
                for e in ROWS_AT.get(n, ()):
                    if e == 0:
                        pe.wait_ge(S["share_t_s"], at(b, 1, 1))
                    else:
                        pe.wait_ge(S["row_s"], at(b, e, EXPERTS))
                    mm(ps[:, BANK_C, :], pick[:, e, :], share_t[:]).then_inc(S["row_mm"], 1)
                if n >= 2:
                    pe.wait_ge(S["hidden_s"], at(b, n - 1, UNITS_E))
                e, k = n // HB, n % HB
                mm(ps[:, BANK_EXP[n % 2], :], w1[:, e, k * P:(k + 1) * P], h_t["d"][:]).then_inc(S["z_mm"], 1)
                if n == 0:
                    for k in range(3):
                        mm(ps[:, BANK_OUT, :], skip_parts[:, k, :], share_t[:], start=(k == 0), stop=False)
                else:
                    down(b, n - 1)

            def expert_sum(b):
                down(b, UNITS_E - 1).then_inc(S["y_mm"], 1)

            def expert_sum_transpose(b):
                pe.wait_ge(S["y_s"], at(b, 1, 1))
                for i in range(NT):
                    last = pe.transpose(ps[:, BANK_A, i * P:(i + 1) * P], moe_t[:, i * P:(i + 1) * P], ident[:])
                last.then_inc(S["yt_mm"], 1)

            pe.wait_ge(S["skip_done"], 1)
            rounds(pe, {
                "pre_t": lambda b: transposes(b, "a", BANK_MAX[0], "ht_a_mm"), "qk_mm": project, "v_mm": project_values,
                "score_max": score_max, "max_t": max_transpose, "score": score, "weigh": weigh_values,
                "head_t": head_transpose, "heads_t": heads_all, "attn_mm": project_out,
                "lora_t": lambda b: transposes(b, "b", BANK_B, "ht_b_mm"), "lora_route": route,
                "lora_outer_t": outer_transpose, "lora_mm": lora_out,
                "wkv_t": lambda b: transposes(b, "c", BANK_B, "xs_mm"), "wkv_k": wkv_keys, "wkv_v": wkv_values,
                "wkv_out": wkv_out,
                "moe_t": lambda b: transposes(b, "d", BANK_C, "ht_d_mm"), "moe_gate": gate, "share_t": share_transpose,
                "expert": expert_block, "expert_sum": expert_sum, "moe_sum_t": expert_sum_transpose})

        @block.vector
        def _(dve):
            dve.wait_ge(S["loaded"], LOADED)
            dve.wait_ge(S["cleared"], 2)
            dve.memset(ones[:], 1.0)
            dve.memset(v_aug[:, :, :, DH:DH + 1], 1.0)
            dve.memset(outer[:, :, LORA_E * RANK:LORA_E * RANK + 1], 1.0)
            dve.tensor_scalar(neg_b1[:], b1[:], -1.0, None, ALU.mult)
            for k in range(3):
                for e in range(EXPERTS):
                    last = dve.tensor_copy(b1_col[:, e * HB:(e + 1) * HB, k * EXPERTS + e], b1[:, e * HB:(e + 1) * HB])
            last.then_inc(S["consts_ready"], 1)
            dve.wait_ge(S["consts_ready"], 1)
            dve.wait_ge(S["td_done"], 1)
            dve.tensor_scalar(td_row[:], ones[:], td[:], None, ALU.mult).then_inc(S["consts_ready"], 1)
            dve.wait_ge(S["skip_mm"], 1)
            R = 3 * EXPERTS
            dve.tensor_tensor(skip[:], ps[0:R, BANK_A, 0:D], b2x3[:], ALU.add).then_inc(S["skip_sum"], 1)
            dve.wait_ge(S["skip_sum"], 1)
            dve.tensor_copy(skip_parts[0:R, 0, :], skip[:]).then_inc(S["skip_hi"], 1)
            dve.wait_ge(S["skip_hi"], 1)
            dve.tensor_tensor(skip_rest[:, 0, :], skip[:], skip_parts[0:R, 0, :], ALU.subtract).then_inc(S["skip_rest"], 1)
            dve.wait_ge(S["skip_rest"], 1)
            dve.tensor_copy(skip_parts[0:R, 1, :], skip_rest[:, 0, :]).then_inc(S["skip_hi"], 1)
            dve.wait_ge(S["skip_hi"], 2)
            dve.tensor_tensor(skip_parts[0:R, 2, :], skip_rest[:, 0, :], skip_parts[0:R, 1, :], ALU.subtract
                              ).then_inc(S["skip_done"], 1)
            dve.memset(maxima[:], 0.0).then_inc(S["s1_used"], 2)
            dve.memset(free_marks[:, 0:1], 1.0).then_inc(S["probs_done"], 2)
            dve.memset(free_marks[:, 2:3], 1.0).then_inc(S["out_stored"], 16)

            def norm_stats(b, n, src):
                for i in range(NT):
                    last = dve.bn_stats(stats[n][:, i, :], src[:, i, :])
                last.then_inc(S[f"stats_{n}"], 1)
                dve.wait_ge(S["loaded"], LOADED)
                dve.wait_ge(S[f"stats_{n}"], at(b, 1, 1))
                for i in range(NT):
                    last = dve.bn_aggr(moments[n][:, i, :], stats[n][:, i, :])
                last.then_inc(S[f"moments_{n}"], 1)

            def normalize(b, n, src, scale=None, ready=None):
                if ready is None:
                    scale = rstd[n]
                    dve.wait_ge(S[f"rstd_{n}"], at(b, 1, 1))
                else:
                    dve.wait_ge(*ready)
                for i in range(NT):
                    last = dve.tensor_scalar(normed[n][:, i, :], src[:, i, :], moments[n][:, i, 0:1],
                                             scale[:, i:i + 1], ALU.subtract, ALU.mult)
                last.then_inc(S[f"normed_{n}"], 1)

            def add_residual(b, n, base, out, done):
                dve.wait_ge(S[f"normed_{n}"], at(b, 1, 1))
                dve.tensor_tensor(out[:], base[:], normed[n][:], ALU.add).then_inc(S[done], 1)
                dve.wait_ge(S[done], at(b, 1, 1))

            def scale_qk(b):
                dve.wait_ge(S["qk_mm"], at(b, 1, 2))
                dve.tensor_scalar(qk[0][:], ps[:, BANK_B, :], bq[:], float(DH) ** -0.5, ALU.add, ALU.mult
                                  ).then_inc(S["qk_scaled"], 1)
                dve.wait_ge(S["qk_mm"], at(b, 2, 2))
                dve.tensor_scalar(qk[1][:], ps[:, BANK_MAX[1], :], bk[:], None, ALU.add).then_inc(S["qk_scaled"], 1)

            def bias_values(b):
                dve.wait_ge(S["v_mm"], at(b, 1, 1))
                for i in range(NT):
                    last = dve.tensor_tensor(v_aug[:, i, :, 0:DH],
                                             ps[:, BANK_MAX[0], i * D:(i + 1) * D].rearrange("p (h d) -> p h d", d=DH),
                                             bv[:].rearrange("p (h d) -> p h d", d=DH), ALU.add)
                last.then_inc(S["v_done"], 1)

            def row_max(b, u):
                g = u // (HG * NT)
                dve.wait_ge(S["s1_ready"], at(b, u + 1, UNITS))
                dve.tensor_reduce(maxima[:, g % 2, u % (HG * NT):u % (HG * NT) + 1], ps[:, BANK_MAX[u % 2], :],
                                  AX.X, ALU.max).then_inc(S["s1_used"], 1)

            def max_parts(b, g):
                src = ps[0:HG * NT, BANK_A, 0:P]
                dve.wait_ge(S["max_mm"], at(b, g + 1, GROUPS))
                if g >= 2:
                    dve.wait_ge(S[f"mrow{g % 2}"], at(b, g // 2, GROUPS // 2) * 32)
                dve.tensor_scalar(max_hi[:, g % 2, :], src, -1.0, None, ALU.mult).then_inc(S["max_hi_s"], 1)
                dve.wait_ge(S["max_hi_s"], at(b, g + 1, GROUPS))
                dve.scalar_tensor_tensor(max_lo[:, g % 2, :], src, -1.0, max_hi[:, g % 2, :], ALU.mult, ALU.subtract
                                         ).then_inc(S["max_lo_s"], 1)

            def head_norm(b, g):
                cols = bank4(BANK_A).rearrange("p t (h c) -> p t h c", c=32)
                dve.wait_ge(S["heads_mm"], at(b, g + 1, GROUPS))
                dve.reciprocal(inv_sum[:], cols[:, :, :, DH]).then_inc(S["inv_s"], 1)
                dve.wait_ge(S["inv_s"], at(b, g + 1, GROUPS))
                dve.tensor_tensor(heads[:, :, HG * g:HG * g + HG, :], cols[:, :, :, 0:DH],
                                  inv_sum[:].unsqueeze(3).to_broadcast([P, NT, HG, DH]), ALU.mult
                                  ).then_inc(S["heads_s"], 1)

            def step_max(b, where):
                s, h4 = where
                u = HG * NT + LEAD + HG * s + h4
                if u < UNITS:
                    row_max(b, u)

            def attn_stats(b):
                dve.wait_ge(S["attn_mm"], at(b, 1, 1))
                for i in range(NT):
                    last = dve.tensor_tensor(attn[:, i, :], ps[:, BANK_A, i * D:(i + 1) * D], bo[:], ALU.add)
                last.then_inc(S["attn_s"], 1)
                dve.wait_ge(S["attn_s"], at(b, 1, 1))
                norm_stats(b, "ao", attn)

            def attn_res(b):
                normalize(b, "ao", attn)
                dve.wait_ge(S["x_skip_loaded"], at(b, 1, 1) * 16)
                add_residual(b, "ao", x_skip, x_attn, "res_a")
                norm_stats(b, "b", x_attn)

            def route_logits(b):
                rm = ps[:, BANK_C, 0:64].rearrange("p (t c) -> p t c", t=NT)
                dve.wait_ge(S["rm_mm"], at(b, 1, 1))
                dve.tensor_tensor(logits[:], rm[:, :, 0:LORA_E],
                                  b_route[:].unsqueeze(1).to_broadcast([P, NT, LORA_E]), ALU.add
                                  ).then_inc(S["logits_s"], 1)
                dve.tensor_scalar(mid[:], rm[:, :, LORA_E:], LORA_SCALE, None, ALU.mult).then_inc(S["mid_s"], 1)
                dve.wait_ge(S["logits_s"], at(b, 1, 1))
                dve.tensor_reduce(route_max[:], logits[:], AX.X, ALU.max).then_inc(S["rmax_s"], 1)
                dve.wait_ge(S["rmax_s"], at(b, 1, 1))
                dve.tensor_tensor(shifted[:], logits[:], route_max[:].unsqueeze(2).to_broadcast([P, NT, LORA_E]),
                                  ALU.subtract).then_inc(S["rshift_s"], 1)

            def route_outer(b):
                dve.wait_ge(S["rexp_s"], at(b, 1, 1))
                dve.tensor_reduce(route_sum[:], route_exp[:], AX.X, ALU.add).then_inc(S["rsum_s"], 1)
                dve.wait_ge(S["rsum_s"], at(b, 1, 1))
                dve.reciprocal(route_inv[:], route_sum[:]).then_inc(S["rinv_s"], 1)
                dve.wait_ge(S["rinv_s"], at(b, 1, 1))
                dve.tensor_tensor(gating[:], route_exp[:], route_inv[:].unsqueeze(2).to_broadcast([P, NT, LORA_E]),
                                  ALU.mult).then_inc(S["gating_s"], 1)
                dve.wait_ge(S["gating_s"], at(b, 1, 1))
                products = outer[:, :, 0:LORA_E * RANK].rearrange("p t (e r) -> p t e r", r=RANK)
                dve.tensor_tensor(products, gating[:].unsqueeze(3).to_broadcast([P, NT, LORA_E, RANK]),
                                  mid[:].unsqueeze(2).to_broadcast([P, NT, LORA_E, RANK]), ALU.mult
                                  ).then_inc(S["outer_s"], 1)

            def lora_stats(b):
                dve.wait_ge(S["lora_mm"], at(b, 1, 1))
                norm_stats(b, "bo", bank4(BANK_B))

            def lora_res(b):
                normalize(b, "bo", bank4(BANK_B))
                add_residual(b, "bo", x_attn, x_res, "res_b")
                norm_stats(b, "c", x_res)

            last_x, x = xs_t[:, 0:SEQ], xs_t[:, 1:]

            def wkv_mix(b):
                dve.wait_ge(S["xs_s"], at(b, 1, 1))
                dve.tensor_tensor(delta[:], x, last_x, ALU.subtract).then_inc(S["delta_s"], 1)
                dve.wait_ge(S["delta_s"], at(b, 1, 1))
                mix(0, mix_k)

            def mix(i, m):
                    dve.scalar_tensor_tensor(mixed[i][:], delta[:], m[:], last_x, ALU.mult, ALU.add
                                             ).then_inc(S["mix_s"], 1)

            def wkv_mix2(b):
                mix(1, mix_v)
                mix(2, mix_r)

            def wkv_scan(b):
                dve.wait_ge(S["expk_s"], at(b, 1, 1))
                dve.wait_ge(S["wkv_v_mm"], at(b, 1, 1))
                dve.tensor_tensor_scan(den[:], td_row[:], exp_k[:], 0.0, ALU.mult, ALU.add).then_inc(S["den_s"], 1)
                dve.tensor_tensor(kv[:], ps[:, BANK_B, :], exp_k[:], ALU.mult).then_inc(S["kv_s"], 1)
                dve.wait_ge(S["kv_s"], at(b, 1, 1))
                dve.tensor_tensor_scan(num[:], td_row[:], kv[:], 0.0, ALU.mult, ALU.add).then_inc(S["num_s"], 1)
                dve.wait_ge(S["den_s"], at(b, 1, 1))
                dve.tensor_scalar(den_eps[:], den[:], WKV_EPS, None, ALU.add).then_inc(S["deneps_s"], 1)

            def wkv_gate(b):
                dve.wait_ge(S["expr_s"], at(b, 1, 1))
                dve.wait_ge(S["deneps_s"], at(b, 1, 1))
                dve.scalar_tensor_tensor(den[:], exp_r[:], 1.0, den_eps[:], ALU.add, ALU.mult).then_inc(S["denr_s"], 1)
                dve.wait_ge(S["denr_s"], at(b, 1, 1))
                dve.reciprocal(den_eps[:], den[:]).then_inc(S["winv_s"], 1)
                dve.wait_ge(S["winv_s"], at(b, 1, 1))
                dve.wait_ge(S["num_s"], at(b, 1, 1))
                dve.tensor_tensor(wkv[:], num[:], den_eps[:], ALU.mult).then_inc(S["wkv_s"], 1)

            def wkv_stats(b):
                dve.wait_ge(S["wkvo_mm"], at(b, 1, 1))
                norm_stats(b, "co", bank4(BANK_B))

            def wkv_res(b):
                normalize(b, "co", bank4(BANK_B))
                add_residual(b, "co", x_res, x_res, "res_c")
                norm_stats(b, "d", x_res)

            wide = [P, NT, EXPERTS]

            def gate_top(b):
                dve.wait_ge(S["gate_mm"], at(b, 1, 1))
                dve.tensor_copy(gates[:], ps[:, BANK_B, 0:NT * EXPERTS].rearrange("p (t e) -> p t e", t=NT)
                                ).then_inc(S["gates_s"], 1)
                dve.wait_ge(S["loaded"], LOADED)
                dve.wait_ge(S["gates_s"], at(b, 1, 1))
                for i in range(NT):
                    last = dve.max(top[:, i, :], gates[:, i, :])
                last.then_inc(S["top_s"], 1)
                dve.wait_ge(S["top_s"], at(b, 1, 1))
                dve.tensor_tensor(gate_sh[:], gates[:], top[:, :, 0:1].to_broadcast(wide), ALU.subtract
                                  ).then_inc(S["gshift_s"], 1)
                dve.tensor_tensor(chosen[:], gates[:], top[:, :, 1:2].to_broadcast(wide), ALU.is_ge
                                  ).then_inc(S["chosen_s"], 1)

            def gate_share(b):
                dve.wait_ge(S["gexp_s"], at(b, 1, 1))
                dve.wait_ge(S["chosen_s"], at(b, 1, 1))
                dve.tensor_tensor(gate_kept[:], gate_exp[:], chosen[:], ALU.mult).then_inc(S["gkept_s"], 1)
                dve.wait_ge(S["gkept_s"], at(b, 1, 1))
                dve.tensor_reduce(gate_sum[:], gate_kept[:], AX.X, ALU.add).then_inc(S["gsum_s"], 1)
                dve.wait_ge(S["gsum_s"], at(b, 1, 1))
                dve.reciprocal(gate_inv[:], gate_sum[:]).then_inc(S["ginv_s"], 1)
                dve.wait_ge(S["ginv_s"], at(b, 1, 1))
                dve.scalar_tensor_tensor(share[:], gate_kept[:], 1.0 / EXPERTS,
                                         gate_inv[:].unsqueeze(2).to_broadcast(wide), ALU.mult, ALU.mult
                                         ).then_inc(S["share_s"], 1)
                dve.wait_ge(S["share_s"], at(b, 1, 1))
                part = [share_parts[:, :, k * EXPERTS:(k + 1) * EXPERTS] for k in range(3)]
                dve.tensor_copy(part[0], share[:]).then_inc(S["shi_s"], 1)
                dve.wait_ge(S["shi_s"], at(b, 1, 1))
                dve.tensor_tensor(share_rest[:], share[:], part[0], ALU.subtract).then_inc(S["srest_s"], 1)
                dve.wait_ge(S["srest_s"], at(b, 1, 1))
                dve.tensor_copy(part[1], share_rest[:]).then_inc(S["smid_s"], 1)
                dve.wait_ge(S["smid_s"], at(b, 1, 1))
                dve.tensor_tensor(part[2], share_rest[:], part[1], ALU.subtract).then_inc(S["slo_s"], 1)

            def hidden_block(b, n):
                e = n // HB
                dve.wait_ge(S["z_mm"], at(b, n + 1, UNITS_E))
                dve.wait_ge(S["row_s"], at(b, e + 1, EXPERTS))
                dve.scalar_tensor_tensor(hidden[:, n % 2, :], ps[:, BANK_EXP[n % 2], :], neg_b1[:, n:n + 1],
                                         share_row[:, e % 2, :], ALU.max, ALU.mult).then_inc(S["hidden_s"], 1)

            def moe_stats(b):
                dve.wait_ge(S["yt_mm"], at(b, 1, 1))
                norm_stats(b, "do", bank4(BANK_A))

            def moe_res(b):
                normalize(b, "do", bank4(BANK_A))
                dve.wait_ge(S["out_stored"], at(b, 1, 1) * 16)
                add_residual(b, "do", x_res, result, "res_d")

            def pre_stats(b):
                dve.wait_ge(S["x_loaded"], at(b, 1, 1) * 16)
                norm_stats(b, "a", x_in)

            rounds(dve, {
                "pre_stats": pre_stats, "pre_norm": lambda b: normalize(b, "a", x_in), "qk_scale": scale_qk,
                "v_bias": bias_values, "score_max": row_max, "score": step_max, "max_t": max_parts,
                "head_norm": head_norm, "head_norm3": lambda b: head_norm(b, GROUPS - 1),
                "attn_stats": attn_stats, "attn_res": attn_res, "lora_norm": lambda b: normalize(b, "b", x_attn),
                "lora_logits": route_logits, "lora_outer": route_outer, "lora_stats": lora_stats, "lora_res": lora_res,
                "wkv_norm": lambda b: normalize(b, "c", x_res, rstd12, (S["c_rstd2"], at(b, 2, 2))),
                "wkv_mix1": wkv_mix, "wkv_k": wkv_mix2, "wkv_scan": wkv_scan, "wkv_gate": wkv_gate,
                "wkv_stats": wkv_stats, "wkv_res": wkv_res,
                "moe_norm": lambda b: normalize(b, "d", x_res), "moe_top": gate_top, "moe_share": gate_share,
                "expert": hidden_block, "moe_sum_stats": moe_stats, "moe_res": moe_res})


_OUT = (BATCH, SEQ, D)


def shape_constants():
    def bits(v):
        return (np.ascontiguousarray(v, dtype=np.float32).view(np.uint32) >> 16).astype(np.uint16)

    slopes = 0.5 ** np.arange(HEADS, dtype=np.float64)
    pos = np.arange(P)
    dist = -np.abs(pos[:, None] - pos[None, :])
    diag = bits(dist[:, None, :] * slopes[None, :, None])
    block, inner = np.arange(SEQ) // P, np.arange(SEQ) % P
    q_rows = np.zeros((CONST_ROWS, HEADS, SEQ))
    k_rows = np.zeros((CONST_ROWS, HEADS, SEQ))
    for r in range(NT):
        q_rows[r] = np.sign(block - r)
        k_rows[r] = slopes[:, None] * (inner * (block == r))
        q_rows[NT + r] = inner * (block == r)
        k_rows[NT + r] = -slopes[:, None] * np.sign(r - block)
        q_rows[2 * NT + r] = -P * np.abs(block - r)
        k_rows[2 * NT + r] = slopes[:, None] * (block == r)
    k_rows[3 * NT:] = 1.0
    pick = np.zeros((P, EXPERTS, P))
    for e in range(EXPERTS):
        for k in range(3):
            pick[k * EXPERTS + e, e, :] = 1.0
    return {"ident": np.eye(P, dtype=np.float32), "identb": bits(np.eye(P)), "diag": diag,
            "q_rows": bits(q_rows), "k_rows": bits(k_rows), "pick": bits(pick)}


def kernel(**inputs):
    import concourse.bacc as bacc
    from concourse.bass_utils import run_bass_kernel_spmd as run

    a = {k: np.asarray(v) for k, v in inputs.items()}
    c = np.ascontiguousarray
    w_heads = a["L0_attn_qkv_w"].reshape(HEADS, 3, DH, D)
    b_heads = a["L0_attn_qkv_b"].reshape(HEADS, 3, DH)
    col = lambda v: c(v.reshape(D, 1))
    arrays = {
        "x": a["L0_attn_x"],
        "wq": c(w_heads[:, 0].reshape(D, D).T), "wk": c(w_heads[:, 1].reshape(D, D).T),
        "wv": c(w_heads[:, 2].reshape(D, D).T), "wo": c(a["L0_attn_out_w"].T),
        "bq": col(b_heads[:, 0]), "bk": col(b_heads[:, 1]), "bv": c(b_heads[:, 2].reshape(D)),
        "bo": a["L0_attn_out_b"],
        "route_w": c(a["L0_ffn_router_w"].T), "route_b": a["L0_ffn_router_b"], "lora_a": a["L0_ffn_lora_A"],
        "lora_b": c(a["L0_ffn_lora_B"].reshape(LORA_E * RANK, D)), "base_w": c(a["L0_ffn_base_w"].T),
        "base_b": a["L0_ffn_base_b"].reshape(1, D),
        "decay": col(a["L1_attn_time_decay"]), "ln_g": col(a["L1_attn_ln_g"]), "ln_b": col(a["L1_attn_ln_b"]),
        "mix_k": col(a["L1_attn_time_mix_k"]), "mix_v": col(a["L1_attn_time_mix_v"]),
        "mix_r": col(a["L1_attn_time_mix_r"]),
        "wkk": c(a["L1_attn_Wk"].T), "wkv": c(a["L1_attn_Wv"].T), "wkr": c(a["L1_attn_Wr"].T),
        "wko": c(a["L1_attn_Wo"].T),
        "w_gate": a["L1_ffn_W_gate"], "w1": a["L1_ffn_W1"], "w2": a["L1_ffn_W2"],
        "b1": c(a["L1_ffn_b1"].reshape(EXPERTS * HB, P).T), "b2": a["L1_ffn_b2"],
    }
    arrays.update(shape_constants())
    nc = bacc.Bacc("TRN2", target_bir_lowering=False, num_devices=1)
    t = {k: nc.dram_tensor(f"in_{k}", v.shape, mybir.dt.from_np(v.dtype), kind="ExternalInput").ap()
         for k, v in arrays.items()}
    t.update({k: t[k].bitcast(BF16) for k in ("identb", "diag", "q_rows", "k_rows", "pick")})
    t["out"] = nc.dram_tensor("out", _OUT, F32, kind="ExternalOutput").ap()
    t["parts"] = nc.dram_tensor("qk_parts_dram", (2, 3, P, SEQ), BF16, kind="Internal").ap()
    layer_norms_attention_lora_wkv_moe_kernel(nc, t)
    r = run(nc, [{f"in_{k}": v for k, v in arrays.items()}], core_ids=[0])
    return r.results[0]["out"]
```

```python
from contextlib import ExitStack

import numpy as np

import concourse.bass as bass
from concourse import mybir

F32 = mybir.dt.float32
BF16 = mybir.dt.bfloat16
ALU = mybir.AluOpType
ACT = mybir.ActivationFunctionType
AX = mybir.AxisListType

P = 128
BATCH, SEQ, D = 8, 512, 128
NT = SEQ // P
HEADS, DH = 16, 8
HG = 4
GROUPS = HEADS // HG
EXPERTS, HID = 8, 512
HB = HID // P
RANK, LORA_E = 8, 8
LORA_SCALE = 16.0 / RANK
EPS = 1e-5
WKV_EPS = 1e-8

SLOTS = [(0, 0), (0, 1), (1, 0), (1, 1), (0, 2), (2, 0)]
BIAS_ROW = DH * len(SLOTS)
MAX_ROW = BIAS_ROW + 3 * NT
CONST_ROWS = 3 * NT + 2

UNITS = HEADS * NT
STEPS = GROUPS * NT

BANK_MAX = (0, 1)
BANK_EXP = (2, 3)
BANK_OUT = 4
BANK_A, BANK_B, BANK_C = 5, 6, 7

EARLY_STEPS = 2
FILL = """lora_mm lora_stats lora_norm_out - lora_res - - wkv_norm wkv_t -
    wkv_mix1 wkv_k wkv_v wkv_den wkv_num wkv_gate wkv_inv - - wkv_out
    wkv_stats wkv_res moe_norm moe_t moe_gate moe_top moe_exp moe_share""".split()
LORA = "lora_t lora_route lora_logits lora_exp lora_outer lora_outer_t".split()
FINISH = ["moe_sum_t", "moe_sum_stats", "moe_res"]
UNITS_E = EXPERTS * HB
BESIDE = {2: ("head_norm3",), 3: ("heads_t",), 4: ("attn_mm",), 5: ("attn_stats",), 7: ("attn_res",),
          9: ("lora_norm",), **{11 + 2 * k: (f,) for k, f in enumerate(LORA)}}
LAST_BESIDE = dict(enumerate((names.split("+") for names in """- - head_norm3 heads_t attn_mm attn_stats attn_res lora_norm
    lora_t lora_route lora_logits lora_exp+lora_outer lora_outer_t lora_mm lora_stats lora_norm_out+lora_res
    - wkv_norm wkv_t wkv_mix1 wkv_k wkv_v wkv_den wkv_num wkv_gate+wkv_inv wkv_out wkv_stats wkv_res
    moe_norm moe_t moe_gate+moe_top moe_exp+moe_share""".split())))
PREPARE = {12: ("pre_stats",), 15: ("pre_norm",), 18: ("pre_t",), 19: ("qk_mm",), 20: ("qk_scale",),
           22: ("v_mm", "qk_hi"), 24: ("qk_mid",), 26: ("store_parts",)}
ROWS_AT = {0: (0,), **{HB * e - 3: (e,) for e in range(1, EXPERTS)}}
FIRST_MAX = 8
MAX_IN_STEP = (2, 2, 3, 3, 4, 4, 4, 4, 3, 3)
UNITS_BEFORE = UNITS - sum(MAX_IN_STEP)
FIRST_GROUP_AT = 22


def timeline(q, i, n):
    yield "loads", i, n
    slots = iter([[(f, q if i is not None else None, None) for f in names.split("+")]
                  + [(p, n, None) for p in PREPARE.get(k, ())] for k, names in enumerate(FILL)])
    for s in range(EARLY_STEPS, STEPS):
        for h4 in range(HG):
            yield "score", i, (s, h4)
            if h4 % 2:
                yield from next(slots)
            if h4 == 1 and s % NT == 1 and s > NT:
                yield "head_t", i, s // NT - 1
        yield from step_end(i, s)
        if q is None and s == EARLY_STEPS:
            yield "down_weights", i, None
    if q is None:
        yield "tables", i, None
    yield "share_t", q, None
    yield "weigh", i, STEPS - 1
    yield "stacks", n, None
    yield "head_out", i, GROUPS - 1
    yield "v_bias", n, None
    u = 0
    for k in range(UNITS_E):
        yield "expert", q, k
        if k == 1:
            yield "head_t", i, GROUPS - 1
        for name in BESIDE.get(k, ()) if n is not None else LAST_BESIDE[k]:
            yield name, i, None
        if k >= FIRST_MAX:
            left = UNITS_BEFORE - u
            for _ in range(min(left, 2 if left > UNITS_E - k else 1)):
                yield "score_max", n, u
                u += 1
            if k == FIRST_GROUP_AT:
                yield "max_t", n, 0
    yield "expert_sum", q, None
    finish = iter([(f, q, None) for f in FINISH])
    for s in range(EARLY_STEPS):
        for h4 in range(HG):
            yield "score", n, (s, h4)
            if h4 % 2 and (f := next(finish, None)):
                yield f
        yield from step_end(n, s)


def step_end(i, s):
    if s > 0:
        yield "weigh", i, s - 1
    if s % NT == 0 and s > 0:
        yield "head_out", i, s // NT - 1
    if s % NT == 1 and s > NT:
        yield "head_norm", i, s // NT - 1
    if s % NT == 2 and s // NT + 1 < GROUPS:
        yield "max_t", i, s // NT + 1


def max_units(s, h4):
    if s >= len(MAX_IN_STEP) or h4 >= MAX_IN_STEP[s]:
        return ()
    return (UNITS_BEFORE + sum(MAX_IN_STEP[:s]) + h4,)


def opening():
    for name in ("first_load", "pre_stats", "pre_norm", "pre_t", "qk_mm", "qk_scale", "v_mm", "qk_hi", "v_bias", "qk_mid",
                 "store_parts", "stacks"):
        yield name, 0, None
    for u in range(UNITS_BEFORE):
        yield "score_max", 0, u
        if u + 1 == HG * NT + 4:
            yield "max_t", 0, 0
            yield "weights", 0, None
    for s in range(EARLY_STEPS):
        for h4 in range(HG):
            yield "score", 0, (s, h4)
        yield from step_end(0, s)


def row_bank(b):
    return BANK_MAX[0] if isinstance(b, int) and b >= BATCH - 2 else BANK_C


def run_pieces(order, pieces):
    for name, seq, arg in order:
        if seq is not None and name in pieces:
            pieces[name](seq, arg) if arg is not None else pieces[name](seq)


def rounds(eng, pieces):
    run_pieces(opening(), pieces)
    run_pieces(timeline(None, 0, 1), pieces)
    with eng.Fori(0, BATCH - 2) as q:
        run_pieces(timeline(q, q + 1, q + 2), pieces)
    run_pieces(timeline(BATCH - 2, BATCH - 1, None), pieces)
    run_pieces(timeline(BATCH - 1, None, None), pieces)


def at(b, k, of):
    return b * of + k


def layer_norms_attention_lora_wkv_moe_kernel(nc, t):
    ctx = ExitStack()
    with ctx:
        def sb(name, shape, dt=F32):
            return ctx.enter_context(nc.sbuf_tensor(name, shape, dt))

        def sem(name):
            return ctx.enter_context(nc.semaphore(name))

        ps = ctx.enter_context(nc.psum_tensor("ps", [P, 8, SEQ], F32))

        def bank4(n, w=D):
            return ps[:, n, 0:NT * w].rearrange("p (t w) -> p t w", t=NT)

        ident = sb("ident", [P, P])
        identb = sb("identb", [P, P], BF16)
        diag = sb("diag", [P, HEADS, P], BF16)
        wq, wk, wv, wo = (sb(n, [P, D]) for n in ("wq", "wk", "wv", "wo"))
        bq, bk = sb("bq", [P, 1]), sb("bk", [P, 1])
        bv, bo = sb("bv", [P, D]), sb("bo", [P, D])
        w_rm = sb("w_rm", [P, LORA_E + RANK])
        b_route = sb("b_route", [P, LORA_E])
        w_base = sb("w_base", [P, D])
        lora_b = sb("lora_b", [P, D])
        decay, ln_g, ln_b = sb("decay", [P, 1]), sb("ln_g", [P, 1]), sb("ln_b", [P, 1])
        mix_k, mix_v, mix_r = sb("mix_k", [P, 1]), sb("mix_v", [P, 1]), sb("mix_r", [P, 1])
        wkk, wkv_, wkr, wko = (sb(n, [P, D]) for n in ("wkk", "wkv_", "wkr", "wko"))
        w_gate = sb("w_gate", [P, EXPERTS])
        w1 = sb("w1", [P, EXPERTS, HID])
        w2 = sb("w2", [P, EXPERTS * HB, D])
        b1 = sb("b1", [P, EXPERTS * HB])
        neg_b1 = sb("neg_b1", [P, EXPERTS * HB])
        b2x3 = sb("b2x3", [3 * EXPERTS, D])
        pick = sb("pick", [P, EXPERTS, P], BF16)
        skip = sb("skip", [3 * EXPERTS, D])
        skip_rest = sb("skip_rest", [3 * EXPERTS, 2, D])
        skip_parts = sb("skip_parts", [P, 3, D], BF16)
        ones = sb("ones", [P, SEQ])
        td = sb("td", [P, 1])
        free_marks = sb("free_marks", [P, 4])
        td_row = sb("td_row", [P, SEQ])
        minus_half = sb("minus_half", [P, NT])
        eps = sb("eps", [P, NT])

        x_in = sb("x_in", [P, NT, D])
        x_skip = sb("x_skip", [P, NT, D])
        x_attn = sb("x_attn", [P, NT, D])
        x_res = sb("x_res", [P, NT, D])
        LN = ("a", "ao", "b", "bo", "c", "co", "d", "do")
        stats = {n: sb(f"stats_{n}", [P, NT, 6]) for n in LN}
        moments = {n: sb(f"moments_{n}", [P, NT, 2]) for n in LN}
        var_eps = {n: sb(f"var_eps_{n}", [P, NT]) for n in LN}
        rstd = {n: sb(f"rstd_{n}", [P, NT]) for n in LN}
        normed = {n: sb(f"normed_{n}", [P, NT, D]) for n in LN}
        h_t = {n: sb(f"h_t_{n}", [P, SEQ]) for n in ("a", "b", "d")}
        qk = [sb(f"qk{i}", [P, SEQ]) for i in range(2)]
        qk_rest = [sb(f"qk_rest{i}", [P, SEQ]) for i in range(2)]
        qk_parts = [sb(f"qk_parts{i}", [P, 3, SEQ], BF16) for i in range(2)]
        q_stack = sb("q_stack", [P, HEADS, SEQ], BF16)
        k_stack = sb("k_stack", [P, HEADS, SEQ], BF16)
        v_aug = sb("v_aug", [P, NT, HEADS, 32])
        maxima = sb("maxima", [P, 2, HG * NT])
        max_hi = sb("max_hi", [HG * NT, 2, P], BF16)
        max_lo = sb("max_lo", [HG * NT, 2, P], BF16)
        probs = sb("probs", [P, 2, HG, SEQ])
        heads_t = sb("heads_t", [P, SEQ])
        inv_sum = sb("inv_sum", [P, NT, HG])
        heads = sb("heads", [P, NT, HEADS, DH])
        heads_all_t = sb("heads_all_t", [P, SEQ])
        attn = sb("attn", [P, NT, D])
        logits = sb("logits", [P, NT, LORA_E])
        route_max = sb("route_max", [P, NT])
        shifted = sb("shifted", [P, NT, LORA_E])
        route_exp = sb("route_exp", [P, NT, LORA_E])
        route_sum = sb("route_sum", [P, NT])
        route_inv = sb("route_inv", [P, NT])
        gating = sb("gating", [P, NT, LORA_E], BF16)
        mid = sb("mid", [P, NT, RANK])
        outer = sb("outer", [P, NT, P])
        outer_t = sb("outer_t", [P, SEQ])
        var1 = sb("var1", [P, NT])
        rstd2 = sb("rstd2", [P, NT])
        rstd12 = sb("rstd12", [P, NT])
        xs_t = sb("xs_t", [P, 1 + SEQ])
        delta = sb("delta", [P, SEQ])
        mixed = [sb(f"mixed{i}", [P, SEQ]) for i in range(3)]
        exp_k = sb("exp_k", [P, SEQ])
        exp_r = sb("exp_r", [P, SEQ])
        kv = sb("kv", [P, SEQ])
        den = sb("den", [P, SEQ])
        num = sb("num", [P, SEQ])
        den_eps = sb("den_eps", [P, SEQ])
        wkv = sb("wkv", [P, SEQ])
        gates = sb("gates", [P, NT, EXPERTS])
        top = sb("top", [P, NT, 8])
        chosen = sb("chosen", [P, NT, EXPERTS])
        gate_sh = sb("gate_sh", [P, NT, EXPERTS])
        gate_exp = sb("gate_exp", [P, NT, EXPERTS])
        gate_kept = sb("gate_kept", [P, NT, EXPERTS])
        gate_sum = sb("gate_sum", [P, NT])
        gate_inv = sb("gate_inv", [P, NT])
        share = sb("share", [P, NT, EXPERTS])
        share_rest = sb("share_rest", [P, NT, EXPERTS])
        share_parts = sb("share_parts", [P, NT, P], BF16)
        share_t = sb("share_t", [P, SEQ], BF16)
        share_row = sb("share_row", [P, 2, SEQ])
        hidden = sb("hidden", [P, 2, SEQ])
        b1_col = hidden[:].rearrange("p k n -> p (k n)")[:, 0:UNITS_E * 3 * EXPERTS].rearrange(
            "p (n c) -> p n c", c=3 * EXPERTS)
        moe_t = sb("moe_t", [P, SEQ])
        result = sb("result", [P, NT, D])

        def normed_t(b, n):
            return h_t["a" if n == "d" and isinstance(b, int) and b == BATCH - 1 else n]

        names = [f"{a}_{n}" for n in LN for a in ("stats", "moments", "vareps", "rstd", "normed")]
        names += """loaded_pre loaded_attn loaded cleared_stacks pool_consts cleared consts_ready skip_mm x_skip_loaded skip_sum skip_hi skip_rest skip_done td_done
            x_loaded out_stored res_a res_b res_c res_d
            ht_a_mm ht_a qk_mm v_mm qk_scaled qk_hi qk_rest1 qk_mid qk_lo v_done parts_stored
            stacks_loaded s1_ready s1_used max_mm max_hi_s max_lo_s mrow0 mrow1
            s2_ready probs_done pv_done heads_t_s heads_mm inv_s heads_s heads_all_mm heads_all_s
            attn_mm attn_s
            ht_b_mm ht_b rm_mm logits_s rmax_s rshift_s rexp_s rsum_s rinv_s gating_s mid_s outer_s
            outer_mm outer_t_s lora_mm
            c_var1 c_vareps2 c_rstd2 xs_mm xs_s delta_s mix_s wkv_k_mm wkv_v_mm wkv_r_mm expk_s expr_s kv_s
            den_s num_s deneps_s denr_s winv_s wkv_s wkvo_mm
            ht_d_mm ht_d gate_mm gates_s top_s chosen_s gshift_s gexp_s gkept_s gsum_s ginv_s share_s
            shi_s srest_s smid_s slo_s share_mm share_t_s row_mm row_s z_mm hidden_s y_mm y_s yt_mm
            """.split()
        S = {n: sem(n) for n in names}

        block = ctx.enter_context(nc.Block())

        loads_pre = [(ident[:], t["ident"]), (wq[:], t["wq"]), (wk[:], t["wk"]), (wv[:], t["wv"]),
                     (bq[:], t["bq"]), (bk[:], t["bk"]), (bv[:], t["bv"].partition_broadcast(P))]
        loads_attn = [
            (q_stack[BIAS_ROW:BIAS_ROW + CONST_ROWS, :, :], t["q_rows"]),
            (k_stack[BIAS_ROW:BIAS_ROW + CONST_ROWS, :, :], t["k_rows"]),
            (identb[:], t["identb"]), (diag[:], t["diag"])]
        loads = [
            (wo[:], t["wo"]), (bo[:], t["bo"].partition_broadcast(P)),
            (w_rm[:, 0:LORA_E], t["route_w"]), (w_rm[:, LORA_E:], t["lora_a"]),
            (b_route[:], t["route_b"].partition_broadcast(P)), (w_base[:], t["base_w"]),
            (lora_b[0:LORA_E * RANK, :], t["lora_b"]), (lora_b[LORA_E * RANK:LORA_E * RANK + 1, :], t["base_b"]),
            (decay[:], t["decay"]), (ln_g[:], t["ln_g"]), (ln_b[:], t["ln_b"]),
            (mix_k[:], t["mix_k"]), (mix_v[:], t["mix_v"]), (mix_r[:], t["mix_r"]),
            (wkk[:], t["wkk"]), (wkv_[:], t["wkv"]), (wkr[:], t["wkr"]), (wko[:], t["wko"]),
            (w_gate[:], t["w_gate"]), (b1[:], t["b1"]),
            (b2x3[0:8, :], t["b2"]), (b2x3[8:16, :], t["b2"]), (b2x3[16:24, :], t["b2"]),
            (pick[:], t["pick"]),
            (w1[:], t["w1"].rearrange("e d h -> d e h")),
        ]
        loads_down = [(w2[:], t["w2"].rearrange("e (n p) d -> p (e n) d", p=P))]
        LOADED_PRE, LOADED_ATTN, LOADED = (16 * len(x) for x in (loads_pre, loads_attn, loads + loads_down))
        SLOT_DMAS = 2 * len(SLOTS) + 1

        def unit(u):
            return u // (HG * NT), u // NT % HG + u // (HG * NT) * HG, u % NT

        @block.sync
        def _(sp):
            def fetch(dst, b, done):
                sp.dma_start(dst[:], t["x"][bass.ds(b, 1), :, :].rearrange("o (t p) d -> p (o t) d", p=P)
                             ).then_inc(S[done], 16)

            def loads_x(i, n=None):
                if i is not None:
                    if not isinstance(i, int) or i > 0:
                        sp.wait_ge(S["res_a"], at(i, 0, 1))
                    fetch(x_skip, i, "x_skip_loaded")
                if n is not None:
                    sp.wait_ge(S["normed_a"], at(n, 0, 1))
                    fetch(x_in, n, "x_loaded")

            def store_parts(b):
                for i, n in ((0, 1), (1, 2)):
                    sp.wait_ge(S["qk_lo"], at(b, n, 2))
                    sp.wait_ge(S["qk_mid"], at(b, n, 2))
                    sp.dma_start(t["parts"][i].rearrange("k p n -> p k n"), qk_parts[i][:]
                                 ).then_inc(S["parts_stored"], 16)

            def build_stacks(b):
                sp.wait_ge(S["parts_stored"], at(b, 1, 1) * 32)
                if not isinstance(b, int) or b > 0:
                    sp.wait_ge(S["pv_done"], at(b - 1, STEPS, STEPS))
                for s, pair in enumerate(SLOTS):
                    for i, stack in ((0, q_stack), (1, k_stack)):
                        sp.dma_start(stack[DH * s:DH * s + DH, :, :],
                                     t["parts"][i, pair[i]].rearrange("(h d) n -> d h n", d=DH)
                                     ).then_inc(S["stacks_loaded"], 16)
                sp.dma_start(q_stack[MAX_ROW:MAX_ROW + 2, :, :], t["q_rows"][3 * NT:3 * NT + 2]
                             ).then_inc(S["stacks_loaded"], 16)

            def max_rows(b, g):
                dst = q_stack[:, HG * g:HG * g + HG, :]
                sp.wait_ge(S["max_lo_s"], at(b, g + 1, GROUPS))
                for k, src in ((0, max_hi), (1, max_lo)):
                    sp.dma_start(dst[MAX_ROW + k:MAX_ROW + k + 1].rearrange("p h (i c) -> p (h i) c", c=P),
                                 src[:, g % 2, :]).then_inc(S[f"mrow{g % 2}"], 16)

            def store(b):
                sp.wait_ge(S["res_d"], at(b, 1, 1))
                sp.dma_start(t["out"][bass.ds(b, 1), :, :].rearrange("o (t p) d -> p (o t) d", p=P), result[:]
                             ).then_inc(S["out_stored"], 16)

            def first_loads(b):
                fetch(x_in, b, "x_loaded")
                for dst, src in loads_pre:
                    sp.dma_start(dst, src).then_inc(S["loaded_pre"], 16)
                sp.wait_ge(S["cleared_stacks"], 2)
                for dst, src in loads_attn:
                    sp.dma_start(dst, src).then_inc(S["loaded_attn"], 16)

            def load_weights(_, part):
                for dst, src in part:
                    sp.dma_start(dst, src).then_inc(S["loaded"], 16)

            rounds(sp, {"first_load": first_loads, "loads": loads_x,
                        "weights": lambda b: load_weights(b, loads), "down_weights": lambda b: load_weights(b, loads_down),
                        "store_parts": store_parts, "stacks": build_stacks, "max_t": max_rows, "moe_res": store})
            sp.wait_ge(S["out_stored"], 16 * (BATCH + 1))

        @block.gpsimd
        def _(pool):
            pool.memset(eps[:], EPS)
            pool.memset(minus_half[:], -0.5).then_inc(S["pool_consts"], 1)
            pool.memset(lora_b[:], 0.0)
            pool.memset(k_stack[:].bitcast(mybir.dt.uint32), 0).then_inc(S["cleared_stacks"], 1)
            pool.memset(v_aug[:], 0.0)
            pool.memset(share_parts[:], 0.0)
            pool.memset(outer[:], 0.0)
            pool.memset(skip_parts[:], 0.0)
            pool.memset(b1_col, 0.0)
            pool.memset(xs_t[:, 0:1], 0.0).then_inc(S["cleared"], 1)
            pool.wait_ge(S["pool_consts"], 1)

            def rsqrt(b, n):
                pool.wait_ge(S[f"moments_{n}"], at(b, 1, 1))
                pool.tensor_tensor(var_eps[n][:], moments[n][:, :, 1], eps[:], ALU.add
                                   ).then_inc(S[f"vareps_{n}"], 1)
                pool.wait_ge(S[f"vareps_{n}"], at(b, 1, 1))
                pool.tensor_tensor(rstd[n][:], var_eps[n][:], minus_half[:], ALU.pow
                                   ).then_inc(S[f"rstd_{n}"], 1)

            def rsqrt_twice(b):
                pool.wait_ge(S["rstd_c"], at(b, 1, 1))
                pool.tensor_tensor(var1[:], moments["c"][:, :, 1], rstd["c"][:], ALU.mult).then_inc(S["c_var1"], 1)
                pool.wait_ge(S["c_var1"], at(b, 1, 2))
                pool.tensor_tensor(var1[:], var1[:], rstd["c"][:], ALU.mult).then_inc(S["c_var1"], 1)
                pool.wait_ge(S["c_var1"], at(b, 2, 2))
                pool.tensor_tensor(var1[:], var1[:], eps[:], ALU.add).then_inc(S["c_vareps2"], 1)
                pool.wait_ge(S["c_vareps2"], at(b, 1, 1))
                pool.tensor_tensor(rstd2[:], var1[:], minus_half[:], ALU.pow).then_inc(S["c_rstd2"], 1)
                pool.wait_ge(S["c_rstd2"], at(b, 1, 2))
                pool.tensor_tensor(rstd12[:], rstd2[:], rstd["c"][:], ALU.mult).then_inc(S["c_rstd2"], 1)

            def split_rest(b):
                for i in range(2):
                    pool.wait_ge(S["qk_hi"], at(b, i + 1, 2))
                    pool.tensor_tensor(qk_rest[i][:], qk[i][:], qk_parts[i][:, 0, :], ALU.subtract
                                       ).then_inc(S["qk_rest1"], 1)

            def split_low(b):
                for i in range(2):
                    pool.wait_ge(S["qk_mid"], at(b, i + 1, 2))
                    pool.tensor_tensor(qk_parts[i][:, 2, :], qk_rest[i][:], qk_parts[i][:, 1, :], ALU.subtract
                                       ).then_inc(S["qk_lo"], 1)

            def lora_res(b):
                rsqrt(b, "c")
                rsqrt_twice(b)

            rounds(pool, {
                "pre_stats": lambda b: rsqrt(b, "a"), "qk_hi": split_rest, "qk_mid": split_low,
                "attn_stats": lambda b: rsqrt(b, "ao"), "attn_res": lambda b: rsqrt(b, "b"),
                "lora_stats": lambda b: rsqrt(b, "bo"), "lora_res": lora_res,
                "wkv_stats": lambda b: rsqrt(b, "co"), "wkv_res": lambda b: rsqrt(b, "d"),
                "moe_sum_stats": lambda b: rsqrt(b, "do")})

        @block.scalar
        def _(act):
            def transposed(b, n):
                act.wait_ge(S[f"ht_{n}_mm"], at(b, 1, 1))
                act.activation(normed_t(b, n)[:], ps[:, {"a": BANK_MAX[0], "b": BANK_B, "d": BANK_C}[n], :], ACT.Copy
                               ).then_inc(S[f"ht_{n}"], 1)

            def high(b):
                for i in range(2):
                    act.wait_ge(S["qk_scaled"], at(b, i + 1, 2))
                    act.activation(qk_parts[i][:, 0, :], qk[i][:], ACT.Copy).then_inc(S["qk_hi"], 1)

            def middle(b):
                for i in range(2):
                    act.wait_ge(S["qk_rest1"], at(b, i + 1, 2))
                    act.activation(qk_parts[i][:, 1, :], qk_rest[i][:], ACT.Copy).then_inc(S["qk_mid"], 1)

            def exps(b, where):
                s, h = where
                if s >= 2 and h == 0:
                    act.wait_ge(S["pv_done"], at(b, s - 1, STEPS))
                n = HG * s + h
                act.wait_ge(S["s2_ready"], at(b, n + 1, UNITS))
                act.activation(probs[:, s % 2, h, :], ps[:, BANK_EXP[n % 2], :], ACT.Exp
                               ).then_inc(S["probs_done"], 1)

            def head_out(b, g):
                act.wait_ge(S["pv_done"], at(b, NT * (g + 1), STEPS))
                act.activation(heads_t[:], ps[:, BANK_OUT, :], ACT.Copy).then_inc(S["heads_t_s"], 1)

            def heads_transposed(b):
                act.wait_ge(S["heads_all_mm"], at(b, 1, 1))
                act.activation(heads_all_t[:], ps[:, BANK_A, :], ACT.Copy).then_inc(S["heads_all_s"], 1)

            def route_exps(b):
                act.wait_ge(S["rshift_s"], at(b, 1, 1))
                act.activation(route_exp[:], shifted[:], ACT.Exp).then_inc(S["rexp_s"], 1)

            def outer_transposed(b):
                act.wait_ge(S["outer_mm"], at(b, 1, 1))
                act.activation(outer_t[:], ps[:, BANK_A, :], ACT.Copy).then_inc(S["outer_t_s"], 1)

            def wkv_transposed(b):
                act.wait_ge(S["xs_mm"], at(b, 1, 1))
                act.activation(xs_t[:, 1:], ps[:, BANK_B, :], ACT.Identity, bias=ln_b[:], scale=ln_g[:]
                               ).then_inc(S["xs_s"], 1)

            def exp_keys(b):
                act.wait_ge(S["wkv_k_mm"], at(b, 1, 1))
                act.activation(exp_k[:], ps[:, BANK_C, :], ACT.Exp).then_inc(S["expk_s"], 1)

            def exp_receptance(b):
                act.wait_ge(S["wkv_r_mm"], at(b, 1, 1))
                act.activation(exp_r[:], ps[:, BANK_C, :], ACT.Exp, scale=-1.0).then_inc(S["expr_s"], 1)

            def gate_exps(b):
                act.wait_ge(S["gshift_s"], at(b, 1, 1))
                act.activation(gate_exp[:], gate_sh[:], ACT.Exp).then_inc(S["gexp_s"], 1)

            def shares_transposed(b):
                act.wait_ge(S["share_mm"], at(b, 1, 1))
                act.activation(share_t[:], ps[:, BANK_B, :].bitcast(BF16)[:, 0:SEQ], ACT.Copy
                               ).then_inc(S["share_t_s"], 1)

            def share_rows(b, k):
                for e in ROWS_AT.get(k, ()):
                    act.wait_ge(S["row_mm"], at(b, e + 1, EXPERTS))
                    if e >= 2:
                        act.wait_ge(S["hidden_s"], at(b, HB * (e - 1), UNITS_E))
                    act.activation(share_row[:, e % 2, :], ps[:, row_bank(b), :], ACT.Copy).then_inc(S["row_s"], 1)

            def expert_sum(b):
                act.wait_ge(S["y_mm"], at(b, 1, 1))
                act.activation(moe_t[:], ps[:, BANK_OUT, :], ACT.Copy).then_inc(S["y_s"], 1)

            def tables(b):
                act.wait_ge(S["loaded"], LOADED)
                act.activation(td[:], decay[:], ACT.Exp).then_inc(S["td_done"], 1)

            rounds(act, {
                "tables": tables,
                "pre_t": lambda b: transposed(b, "a"), "qk_hi": high, "qk_mid": middle, "score": exps,
                "head_out": head_out, "heads_t": heads_transposed,
                "lora_t": lambda b: transposed(b, "b"), "lora_exp": route_exps, "lora_outer_t": outer_transposed,
                "wkv_t": wkv_transposed, "wkv_k": exp_keys, "wkv_v": exp_receptance,
                "moe_t": lambda b: transposed(b, "d"), "moe_exp": gate_exps, "share_t": shares_transposed,
                "expert": share_rows, "expert_sum": expert_sum})

        @block.tensor
        def _(pe):
            def mm(out, lhs, rhs, start=True, stop=True, **kw):
                return pe.matmul(out, lhs, rhs, start=start, stop=stop, skip_group_check=True, **kw)

            def tables(b):
                pe.wait_ge(S["loaded"], LOADED)
                pe.wait_ge(S["consts_ready"], 1)
                for n in range(EXPERTS * HB):
                    last = mm(ps[0:3 * EXPERTS, BANK_B, 0:D], b1_col[:, n, :], w2[:, n, :],
                              start=(n == 0), stop=(n == EXPERTS * HB - 1))
                last.then_inc(S["skip_mm"], 1)

            def transposes(b, n, bank, done):
                if isinstance(b, int) and b == 0:
                    pe.wait_ge(S["loaded_pre"], LOADED_PRE)
                pe.wait_ge(S[f"normed_{n}"], at(b, 1, 1))
                for i in range(NT):
                    last = pe.transpose(ps[:, bank, i * P:(i + 1) * P], normed[n][:, i, :], ident[:])
                last.then_inc(S[done], 1)

            def project(b):
                pe.wait_ge(S["ht_a"], at(b, 1, 1))
                if not isinstance(b, int) or b > 0:
                    pe.wait_ge(S["max_lo_s"], at(b - 1, GROUPS, GROUPS))
                mm(ps[:, BANK_MAX[1], :], wq[:], h_t["a"][:]).then_inc(S["qk_mm"], 1)
                mm(ps[:, BANK_A, :], wk[:], h_t["a"][:]).then_inc(S["qk_mm"], 1)

            def project_values(b):
                pe.wait_ge(S["qk_scaled"], at(b, 2, 2))
                for i in range(NT):
                    last = mm(ps[:, BANK_MAX[0], i * D:(i + 1) * D], h_t["a"][:, i * P:(i + 1) * P], wv[:])
                last.then_inc(S["v_mm"], 1)

            def score_max(b, u):
                _, h, i = unit(u)
                bank = ps[:, BANK_MAX[u % 2], :]
                if u == 0:
                    if isinstance(b, int) and b == 0:
                        pe.wait_ge(S["loaded_attn"], LOADED_ATTN)
                    pe.wait_ge(S["stacks_loaded"], at(b, 1, 1) * 16 * SLOT_DMAS)
                    pe.wait_ge(S["v_done"], at(b, 1, 1))
                pe.wait_ge(S["s1_used"], at(b, u + 1, UNITS))
                mm(bank, q_stack[:, h, i * P:(i + 1) * P], k_stack[:, h, :], stop=False)
                mm(bank[:, i * P:(i + 1) * P], identb[:], diag[:, h, :], start=False
                   ).then_inc(S["s1_ready"], 1)

            def max_transpose(b, g):
                pe.wait_ge(S["s1_used"], at(b, 2 + (g + 1) * HG * NT, UNITS))
                if g == 0 and (not isinstance(b, int) or b > 0):
                    pe.wait_ge(S["outer_t_s"], at(b - 1, 1, 1))
                if g >= 2:
                    pe.wait_ge(S["heads_s"], at(b, g - 1, GROUPS))
                pe.transpose(ps[0:HG * NT, BANK_A, 0:P], maxima[:, g % 2, :], ident[:]).then_inc(S["max_mm"], 1)

            def score(b, where):
                s, h4 = where
                for u in max_units(s, h4):
                    score_max(b, u)
                g, j = s // NT, s % NT
                h, n = HG * g + h4, HG * s + h4
                if j == 0 and h4 == 0:
                    pe.wait_ge(S[f"mrow{g % 2}"], at(b, g // 2 + 1, GROUPS // 2) * 32)
                pe.wait_ge(S["probs_done"], at(b, n + 1, UNITS))
                bank = ps[:, BANK_EXP[n % 2], :]
                mm(bank, k_stack[:, h, j * P:(j + 1) * P], q_stack[:, h, :], stop=False)
                mm(bank[:, j * P:(j + 1) * P], identb[:], diag[:, h, :], start=False
                   ).then_inc(S["s2_ready"], 1)

            def weigh_values(b, s):
                g, j = s // NT, s % NT
                pe.wait_ge(S["probs_done"], at(b, 2 + HG * (s + 1), UNITS))
                if j == 0 and g > 0:
                    pe.wait_ge(S["heads_t_s"], at(b, g, GROUPS))
                for r in range(HG):
                    last = mm(ps[32 * r:32 * r + 32, BANK_OUT, :], v_aug[:, j, HG * g + r, :],
                              probs[:, s % 2, r, :], start=(j == 0), stop=(j == NT - 1), tile_position=(0, 32 * r))
                last.then_inc(S["pv_done"], 1)

            def head_transpose(b, g):
                pe.wait_ge(S["heads_t_s"], at(b, g + 1, GROUPS))
                if g > 0:
                    pe.wait_ge(S["heads_s"], at(b, g, GROUPS))
                if g < GROUPS - 1:
                    pe.wait_ge(S["max_lo_s"], at(b, g + 2, GROUPS))
                for i in range(NT):
                    last = pe.transpose(ps[:, BANK_A, i * P:(i + 1) * P], heads_t[:, i * P:(i + 1) * P], ident[:])
                last.then_inc(S["heads_mm"], 1)

            def heads_all(b):
                pe.wait_ge(S["heads_s"], at(b, GROUPS, GROUPS))
                for i in range(NT):
                    last = pe.transpose(ps[:, BANK_A, i * P:(i + 1) * P],
                                        heads[:, i, :, :].rearrange("p h d -> p (h d)"), ident[:])
                last.then_inc(S["heads_all_mm"], 1)

            def project_out(b):
                pe.wait_ge(S["heads_all_s"], at(b, 1, 1))
                for i in range(NT):
                    last = mm(ps[:, BANK_A, i * D:(i + 1) * D], heads_all_t[:, i * P:(i + 1) * P], wo[:])
                last.then_inc(S["attn_mm"], 1)

            def route(b):
                pe.wait_ge(S["ht_b"], at(b, 1, 1))
                for i in range(NT):
                    last = mm(ps[:, BANK_A, i * 16:(i + 1) * 16], h_t["b"][:, i * P:(i + 1) * P], w_rm[:])
                last.then_inc(S["rm_mm"], 1)

            def outer_transpose(b):
                pe.wait_ge(S["outer_s"], at(b, 1, 1))
                for i in range(NT):
                    last = pe.transpose(ps[:, BANK_A, i * P:(i + 1) * P], outer[:, i, :], ident[:])
                last.then_inc(S["outer_mm"], 1)

            def lora_out(b):
                pe.wait_ge(S["outer_t_s"], at(b, 1, 1))
                for i in range(NT):
                    out = ps[:, BANK_B, i * D:(i + 1) * D]
                    mm(out, h_t["b"][:, i * P:(i + 1) * P], w_base[:], stop=False)
                    last = mm(out, outer_t[:, i * P:(i + 1) * P], lora_b[:], start=False)
                last.then_inc(S["lora_mm"], 1)

            def wkv_keys(b):
                pe.wait_ge(S["mix_s"], at(b, 1, 3))
                mm(ps[:, BANK_C, :], wkk[:], mixed[0][:]).then_inc(S["wkv_k_mm"], 1)

            def wkv_values(b):
                pe.wait_ge(S["mix_s"], at(b, 2, 3))
                mm(ps[:, BANK_B, :], wkv_[:], mixed[1][:]).then_inc(S["wkv_v_mm"], 1)
                pe.wait_ge(S["mix_s"], at(b, 3, 3))
                pe.wait_ge(S["expk_s"], at(b, 1, 1))
                mm(ps[:, BANK_C, :], wkr[:], mixed[2][:]).then_inc(S["wkv_r_mm"], 1)

            def wkv_out(b):
                pe.wait_ge(S["wkv_s"], at(b, 1, 1))
                for i in range(NT):
                    last = mm(ps[:, BANK_B, i * D:(i + 1) * D], wkv[:, i * P:(i + 1) * P], wko[:])
                last.then_inc(S["wkvo_mm"], 1)

            def gate(b):
                pe.wait_ge(S["ht_d"], at(b, 1, 1))
                for i in range(NT):
                    last = mm(ps[:, BANK_B, i * EXPERTS:(i + 1) * EXPERTS], normed_t(b, "d")[:, i * P:(i + 1) * P], w_gate[:])
                last.then_inc(S["gate_mm"], 1)

            def share_transpose(b):
                pe.wait_ge(S["slo_s"], at(b, 1, 1))
                pe.wait_ge(S["smid_s"], at(b, 1, 1))
                shares = ps[:, BANK_B, :].bitcast(BF16)
                for i in range(NT):
                    last = pe.transpose(shares[:, i * P:(i + 1) * P], share_parts[:, i, :], identb[:])
                last.then_inc(S["share_mm"], 1)

            def down(b, n):
                pe.wait_ge(S["hidden_s"], at(b, n + 1, UNITS_E))
                return mm(ps[:, BANK_OUT, :], w2[:, n, :], hidden[:, n % 2, :], start=False, stop=(n == UNITS_E - 1))

            def expert_block(b, n):
                for e in ROWS_AT.get(n, ()):
                    if e == 0:
                        pe.wait_ge(S["share_t_s"], at(b, 1, 1))
                    else:
                        pe.wait_ge(S["row_s"], at(b, e, EXPERTS))
                    mm(ps[:, row_bank(b), :], pick[:, e, :], share_t[:]).then_inc(S["row_mm"], 1)
                if n >= 2:
                    pe.wait_ge(S["hidden_s"], at(b, n - 1, UNITS_E))
                e, k = n // HB, n % HB
                mm(ps[:, BANK_EXP[n % 2], :], w1[:, e, k * P:(k + 1) * P], normed_t(b, "d")[:]).then_inc(S["z_mm"], 1)
                if n == 0:
                    if not isinstance(b, int) or b < BATCH - 1:
                        pe.wait_ge(S["heads_t_s"], at(b + 1, GROUPS, GROUPS))
                    for k in range(3):
                        mm(ps[:, BANK_OUT, :], skip_parts[:, k, :], share_t[:], start=(k == 0), stop=False)
                else:
                    down(b, n - 1)

            def expert_sum(b):
                down(b, UNITS_E - 1).then_inc(S["y_mm"], 1)

            def expert_sum_transpose(b):
                pe.wait_ge(S["y_s"], at(b, 1, 1))
                for i in range(NT):
                    last = pe.transpose(ps[:, BANK_A, i * P:(i + 1) * P], moe_t[:, i * P:(i + 1) * P], ident[:])
                last.then_inc(S["yt_mm"], 1)

            rounds(pe, {
                "tables": tables,
                "pre_t": lambda b: transposes(b, "a", BANK_MAX[0], "ht_a_mm"), "qk_mm": project, "v_mm": project_values,
                "score_max": score_max, "max_t": max_transpose, "score": score, "weigh": weigh_values,
                "head_t": head_transpose, "heads_t": heads_all, "attn_mm": project_out,
                "lora_t": lambda b: transposes(b, "b", BANK_B, "ht_b_mm"), "lora_route": route,
                "lora_outer_t": outer_transpose, "lora_mm": lora_out,
                "wkv_t": lambda b: transposes(b, "c", BANK_B, "xs_mm"), "wkv_k": wkv_keys, "wkv_v": wkv_values,
                "wkv_out": wkv_out,
                "moe_t": lambda b: transposes(b, "d", BANK_C, "ht_d_mm"), "moe_gate": gate, "share_t": share_transpose,
                "expert": expert_block, "expert_sum": expert_sum, "moe_sum_t": expert_sum_transpose})

        @block.vector
        def _(dve):
            dve.memset(q_stack[:].bitcast(mybir.dt.uint32), 0).then_inc(S["cleared_stacks"], 1)

            def tables(b):
                dve.wait_ge(S["loaded"], LOADED)
                dve.wait_ge(S["cleared"], 1)
                dve.memset(ones[:], 1.0)
                dve.memset(outer[:, :, LORA_E * RANK:LORA_E * RANK + 1], 1.0)
                dve.tensor_scalar(neg_b1[:], b1[:], -1.0, None, ALU.mult)
                for k in range(3):
                    for e in range(EXPERTS):
                        last = dve.tensor_copy(b1_col[:, e * HB:(e + 1) * HB, k * EXPERTS + e], b1[:, e * HB:(e + 1) * HB])
                last.then_inc(S["consts_ready"], 1)
                dve.wait_ge(S["consts_ready"], 1)
                dve.wait_ge(S["td_done"], 1)
                dve.tensor_scalar(td_row[:], ones[:], td[:], None, ALU.mult).then_inc(S["consts_ready"], 1)
                dve.wait_ge(S["skip_mm"], 1)
                R = 3 * EXPERTS
                dve.tensor_tensor(skip[:], ps[0:R, BANK_B, 0:D], b2x3[:], ALU.add).then_inc(S["skip_sum"], 1)
                dve.wait_ge(S["skip_sum"], 1)
                dve.tensor_copy(skip_parts[0:R, 0, :], skip[:]).then_inc(S["skip_hi"], 1)
                dve.wait_ge(S["skip_hi"], 1)
                dve.tensor_tensor(skip_rest[:, 0, :], skip[:], skip_parts[0:R, 0, :], ALU.subtract
                                  ).then_inc(S["skip_rest"], 1)
                dve.wait_ge(S["skip_rest"], 1)
                dve.tensor_copy(skip_parts[0:R, 1, :], skip_rest[:, 0, :]).then_inc(S["skip_hi"], 1)
                dve.wait_ge(S["skip_hi"], 2)
                dve.tensor_tensor(skip_parts[0:R, 2, :], skip_rest[:, 0, :], skip_parts[0:R, 1, :], ALU.subtract
                                  ).then_inc(S["skip_done"], 1)

            dve.memset(maxima[:], 0.0).then_inc(S["s1_used"], 2)
            dve.memset(free_marks[:, 0:1], 1.0).then_inc(S["probs_done"], 2)
            dve.memset(free_marks[:, 2:3], 1.0).then_inc(S["out_stored"], 16)

            def residual(b):
                return x_in if isinstance(b, int) and b == BATCH - 1 else x_res

            def norm_stats(b, n, src):
                for i in range(NT):
                    last = dve.bn_stats(stats[n][:, i, :], src[:, i, :])
                last.then_inc(S[f"stats_{n}"], 1)
                dve.wait_ge(S["loaded_pre"], LOADED_PRE)
                dve.wait_ge(S[f"stats_{n}"], at(b, 1, 1))
                for i in range(NT):
                    last = dve.bn_aggr(moments[n][:, i, :], stats[n][:, i, :])
                last.then_inc(S[f"moments_{n}"], 1)

            def normalize(b, n, src, scale=None, ready=None):
                if ready is None:
                    scale = rstd[n]
                    dve.wait_ge(S[f"rstd_{n}"], at(b, 1, 1))
                else:
                    dve.wait_ge(*ready)
                for i in range(NT):
                    last = dve.tensor_scalar(normed[n][:, i, :], src[:, i, :], moments[n][:, i, 0:1],
                                             scale[:, i:i + 1], ALU.subtract, ALU.mult)
                last.then_inc(S[f"normed_{n}"], 1)

            def add_residual(b, n, base, out, done):
                dve.wait_ge(S[f"normed_{n}"], at(b, 1, 1))
                dve.tensor_tensor(out[:], base[:], normed[n][:], ALU.add).then_inc(S[done], 1)
                dve.wait_ge(S[done], at(b, 1, 1))

            def scale_qk(b):
                dve.wait_ge(S["qk_mm"], at(b, 1, 2))
                dve.tensor_scalar(qk[0][:], ps[:, BANK_MAX[1], :], bq[:], float(DH) ** -0.5, ALU.add, ALU.mult
                                  ).then_inc(S["qk_scaled"], 1)
                dve.wait_ge(S["qk_mm"], at(b, 2, 2))
                dve.tensor_scalar(qk[1][:], ps[:, BANK_A, :], bk[:], None, ALU.add).then_inc(S["qk_scaled"], 1)

            def bias_values(b):
                if isinstance(b, int) and b == 0:
                    dve.wait_ge(S["cleared"], 1)
                    dve.memset(v_aug[:, :, :, DH:DH + 1], 1.0)
                else:
                    dve.wait_ge(S["pv_done"], at(b - 1, STEPS, STEPS))
                dve.wait_ge(S["v_mm"], at(b, 1, 1))
                for i in range(NT):
                    last = dve.tensor_tensor(v_aug[:, i, :, 0:DH],
                                             ps[:, BANK_MAX[0], i * D:(i + 1) * D].rearrange("p (h d) -> p h d", d=DH),
                                             bv[:].rearrange("p (h d) -> p h d", d=DH), ALU.add)
                last.then_inc(S["v_done"], 1)

            def row_max(b, u):
                g = u // (HG * NT)
                dve.wait_ge(S["s1_ready"], at(b, u + 1, UNITS))
                dve.tensor_reduce(maxima[:, g % 2, u % (HG * NT):u % (HG * NT) + 1], ps[:, BANK_MAX[u % 2], :],
                                  AX.X, ALU.max).then_inc(S["s1_used"], 1)

            def max_parts(b, g):
                src = ps[0:HG * NT, BANK_A, 0:P]
                dve.wait_ge(S["max_mm"], at(b, g + 1, GROUPS))
                if g >= 2:
                    dve.wait_ge(S[f"mrow{g % 2}"], at(b, g // 2, GROUPS // 2) * 32)
                dve.tensor_scalar(max_hi[:, g % 2, :], src, -1.0, None, ALU.mult).then_inc(S["max_hi_s"], 1)
                dve.wait_ge(S["max_hi_s"], at(b, g + 1, GROUPS))
                dve.scalar_tensor_tensor(max_lo[:, g % 2, :], src, -1.0, max_hi[:, g % 2, :], ALU.mult, ALU.subtract
                                         ).then_inc(S["max_lo_s"], 1)

            def head_norm(b, g):
                cols = bank4(BANK_A).rearrange("p t (h c) -> p t h c", c=32)
                dve.wait_ge(S["heads_mm"], at(b, g + 1, GROUPS))
                dve.reciprocal(inv_sum[:], cols[:, :, :, DH]).then_inc(S["inv_s"], 1)
                dve.wait_ge(S["inv_s"], at(b, g + 1, GROUPS))
                dve.tensor_tensor(heads[:, :, HG * g:HG * g + HG, :], cols[:, :, :, 0:DH],
                                  inv_sum[:].unsqueeze(3).to_broadcast([P, NT, HG, DH]), ALU.mult
                                  ).then_inc(S["heads_s"], 1)

            def step_max(b, where):
                s, h4 = where
                for u in max_units(s, h4):
                    row_max(b, u)

            def attn_stats(b):
                dve.wait_ge(S["attn_mm"], at(b, 1, 1))
                for i in range(NT):
                    last = dve.tensor_tensor(attn[:, i, :], ps[:, BANK_A, i * D:(i + 1) * D], bo[:], ALU.add)
                last.then_inc(S["attn_s"], 1)
                dve.wait_ge(S["attn_s"], at(b, 1, 1))
                norm_stats(b, "ao", attn)

            def attn_res(b):
                normalize(b, "ao", attn)
                dve.wait_ge(S["x_skip_loaded"], at(b, 1, 1) * 16)
                add_residual(b, "ao", x_skip, x_attn, "res_a")
                norm_stats(b, "b", x_attn)

            def route_logits(b):
                rm = ps[:, BANK_A, 0:64].rearrange("p (t c) -> p t c", t=NT)
                dve.wait_ge(S["rm_mm"], at(b, 1, 1))
                dve.tensor_tensor(logits[:], rm[:, :, 0:LORA_E],
                                  b_route[:].unsqueeze(1).to_broadcast([P, NT, LORA_E]), ALU.add
                                  ).then_inc(S["logits_s"], 1)
                dve.tensor_scalar(mid[:], rm[:, :, LORA_E:], LORA_SCALE, None, ALU.mult).then_inc(S["mid_s"], 1)
                dve.wait_ge(S["logits_s"], at(b, 1, 1))
                dve.tensor_reduce(route_max[:], logits[:], AX.X, ALU.max).then_inc(S["rmax_s"], 1)
                dve.wait_ge(S["rmax_s"], at(b, 1, 1))
                dve.tensor_tensor(shifted[:], logits[:], route_max[:].unsqueeze(2).to_broadcast([P, NT, LORA_E]),
                                  ALU.subtract).then_inc(S["rshift_s"], 1)

            def route_outer(b):
                dve.wait_ge(S["rexp_s"], at(b, 1, 1))
                dve.tensor_reduce(route_sum[:], route_exp[:], AX.X, ALU.add).then_inc(S["rsum_s"], 1)
                dve.wait_ge(S["rsum_s"], at(b, 1, 1))
                dve.reciprocal(route_inv[:], route_sum[:]).then_inc(S["rinv_s"], 1)
                dve.wait_ge(S["rinv_s"], at(b, 1, 1))
                dve.tensor_tensor(gating[:], route_exp[:], route_inv[:].unsqueeze(2).to_broadcast([P, NT, LORA_E]),
                                  ALU.mult).then_inc(S["gating_s"], 1)
                dve.wait_ge(S["gating_s"], at(b, 1, 1))
                products = outer[:, :, 0:LORA_E * RANK].rearrange("p t (e r) -> p t e r", r=RANK)
                dve.tensor_tensor(products, gating[:].unsqueeze(3).to_broadcast([P, NT, LORA_E, RANK]),
                                  mid[:].unsqueeze(2).to_broadcast([P, NT, LORA_E, RANK]), ALU.mult
                                  ).then_inc(S["outer_s"], 1)

            def lora_stats(b):
                dve.wait_ge(S["lora_mm"], at(b, 1, 1))
                norm_stats(b, "bo", bank4(BANK_B))

            def lora_res(b):
                add_residual(b, "bo", x_attn, residual(b), "res_b")
                norm_stats(b, "c", residual(b))

            last_x, x = xs_t[:, 0:SEQ], xs_t[:, 1:]

            def wkv_mix(b):
                dve.wait_ge(S["xs_s"], at(b, 1, 1))
                dve.tensor_tensor(delta[:], x, last_x, ALU.subtract).then_inc(S["delta_s"], 1)
                dve.wait_ge(S["delta_s"], at(b, 1, 1))
                mix(0, mix_k)

            def mix(i, m):
                dve.scalar_tensor_tensor(mixed[i][:], delta[:], m[:], last_x, ALU.mult, ALU.add
                                         ).then_inc(S["mix_s"], 1)

            def wkv_mix2(b):
                mix(1, mix_v)
                mix(2, mix_r)

            def wkv_den(b):
                dve.wait_ge(S["expk_s"], at(b, 1, 1))
                dve.wait_ge(S["wkv_v_mm"], at(b, 1, 1))
                dve.tensor_tensor_scan(den[:], td_row[:], exp_k[:], 0.0, ALU.mult, ALU.add).then_inc(S["den_s"], 1)
                dve.tensor_tensor(kv[:], ps[:, BANK_B, :], exp_k[:], ALU.mult).then_inc(S["kv_s"], 1)

            def wkv_num(b):
                dve.wait_ge(S["kv_s"], at(b, 1, 1))
                dve.tensor_tensor_scan(num[:], td_row[:], kv[:], 0.0, ALU.mult, ALU.add).then_inc(S["num_s"], 1)
                dve.wait_ge(S["den_s"], at(b, 1, 1))
                dve.tensor_scalar(den_eps[:], den[:], WKV_EPS, None, ALU.add).then_inc(S["deneps_s"], 1)

            def wkv_gate(b):
                dve.wait_ge(S["expr_s"], at(b, 1, 1))
                dve.wait_ge(S["deneps_s"], at(b, 1, 1))
                dve.scalar_tensor_tensor(den[:], exp_r[:], 1.0, den_eps[:], ALU.add, ALU.mult).then_inc(S["denr_s"], 1)

            def wkv_inverse(b):
                dve.wait_ge(S["denr_s"], at(b, 1, 1))
                dve.reciprocal(den_eps[:], den[:]).then_inc(S["winv_s"], 1)
                dve.wait_ge(S["winv_s"], at(b, 1, 1))
                dve.wait_ge(S["num_s"], at(b, 1, 1))
                dve.tensor_tensor(wkv[:], num[:], den_eps[:], ALU.mult).then_inc(S["wkv_s"], 1)

            def wkv_stats(b):
                dve.wait_ge(S["wkvo_mm"], at(b, 1, 1))
                norm_stats(b, "co", bank4(BANK_B))

            def wkv_res(b):
                normalize(b, "co", bank4(BANK_B))
                add_residual(b, "co", residual(b), residual(b), "res_c")
                norm_stats(b, "d", residual(b))

            wide = [P, NT, EXPERTS]

            def gate_top(b):
                dve.wait_ge(S["gate_mm"], at(b, 1, 1))
                dve.tensor_copy(gates[:], ps[:, BANK_B, 0:NT * EXPERTS].rearrange("p (t e) -> p t e", t=NT)
                                ).then_inc(S["gates_s"], 1)
                dve.wait_ge(S["loaded_pre"], LOADED_PRE)
                dve.wait_ge(S["gates_s"], at(b, 1, 1))
                for i in range(NT):
                    last = dve.max(top[:, i, :], gates[:, i, :])
                last.then_inc(S["top_s"], 1)
                dve.wait_ge(S["top_s"], at(b, 1, 1))
                dve.tensor_tensor(gate_sh[:], gates[:], top[:, :, 0:1].to_broadcast(wide), ALU.subtract
                                  ).then_inc(S["gshift_s"], 1)
                dve.tensor_tensor(chosen[:], gates[:], top[:, :, 1:2].to_broadcast(wide), ALU.is_ge
                                  ).then_inc(S["chosen_s"], 1)

            def gate_share(b):
                dve.wait_ge(S["gexp_s"], at(b, 1, 1))
                dve.wait_ge(S["chosen_s"], at(b, 1, 1))
                dve.tensor_tensor(gate_kept[:], gate_exp[:], chosen[:], ALU.mult).then_inc(S["gkept_s"], 1)
                dve.wait_ge(S["gkept_s"], at(b, 1, 1))
                dve.tensor_reduce(gate_sum[:], gate_kept[:], AX.X, ALU.add).then_inc(S["gsum_s"], 1)
                dve.wait_ge(S["gsum_s"], at(b, 1, 1))
                dve.reciprocal(gate_inv[:], gate_sum[:]).then_inc(S["ginv_s"], 1)
                dve.wait_ge(S["ginv_s"], at(b, 1, 1))
                dve.scalar_tensor_tensor(share[:], gate_kept[:], 1.0 / EXPERTS,
                                         gate_inv[:].unsqueeze(2).to_broadcast(wide), ALU.mult, ALU.mult
                                         ).then_inc(S["share_s"], 1)
                dve.wait_ge(S["share_s"], at(b, 1, 1))
                part = [share_parts[:, :, k * EXPERTS:(k + 1) * EXPERTS] for k in range(3)]
                dve.tensor_copy(part[0], share[:]).then_inc(S["shi_s"], 1)
                dve.wait_ge(S["shi_s"], at(b, 1, 1))
                dve.tensor_tensor(share_rest[:], share[:], part[0], ALU.subtract).then_inc(S["srest_s"], 1)
                dve.wait_ge(S["srest_s"], at(b, 1, 1))
                dve.tensor_copy(part[1], share_rest[:]).then_inc(S["smid_s"], 1)
                dve.wait_ge(S["smid_s"], at(b, 1, 1))
                dve.tensor_tensor(part[2], share_rest[:], part[1], ALU.subtract).then_inc(S["slo_s"], 1)

            def hidden_block(b, n):
                e = n // HB
                dve.wait_ge(S["z_mm"], at(b, n + 1, UNITS_E))
                dve.wait_ge(S["row_s"], at(b, e + 1, EXPERTS))
                dve.scalar_tensor_tensor(hidden[:, n % 2, :], ps[:, BANK_EXP[n % 2], :], neg_b1[:, n:n + 1],
                                         share_row[:, e % 2, :], ALU.max, ALU.mult).then_inc(S["hidden_s"], 1)

            def moe_stats(b):
                dve.wait_ge(S["yt_mm"], at(b, 1, 1))
                norm_stats(b, "do", bank4(BANK_A))

            def moe_res(b):
                normalize(b, "do", bank4(BANK_A))
                dve.wait_ge(S["out_stored"], at(b, 1, 1) * 16)
                add_residual(b, "do", residual(b), result, "res_d")

            def pre_stats(b):
                dve.wait_ge(S["x_loaded"], at(b, 1, 1) * 16)
                norm_stats(b, "a", x_in)

            rounds(dve, {
                "tables": tables,
                "pre_stats": pre_stats, "pre_norm": lambda b: normalize(b, "a", x_in), "qk_scale": scale_qk,
                "v_bias": bias_values, "score_max": row_max, "score": step_max, "max_t": max_parts,
                "head_norm": head_norm, "head_norm3": lambda b: head_norm(b, GROUPS - 1),
                "attn_stats": attn_stats, "attn_res": attn_res, "lora_norm": lambda b: normalize(b, "b", x_attn),
                "lora_logits": route_logits, "lora_outer": route_outer, "lora_stats": lora_stats, "lora_res": lora_res,
                "wkv_norm": lambda b: normalize(b, "c", residual(b), rstd12, (S["c_rstd2"], at(b, 2, 2))),
                "wkv_mix1": wkv_mix, "wkv_k": wkv_mix2, "wkv_den": wkv_den, "wkv_num": wkv_num, "wkv_gate": wkv_gate, "wkv_inv": wkv_inverse,
                "lora_norm_out": lambda b: normalize(b, "bo", bank4(BANK_B)),
                "wkv_stats": wkv_stats, "wkv_res": wkv_res,
                "moe_norm": lambda b: normalize(b, "d", residual(b)), "moe_top": gate_top, "moe_share": gate_share,
                "expert": hidden_block, "moe_sum_stats": moe_stats, "moe_res": moe_res})


_OUT = (BATCH, SEQ, D)


def shape_constants():
    def bits(v):
        return (np.ascontiguousarray(v, dtype=np.float32).view(np.uint32) >> 16).astype(np.uint16)

    slopes = 0.5 ** np.arange(HEADS, dtype=np.float64)
    pos = np.arange(P)
    dist = -np.abs(pos[:, None] - pos[None, :])
    diag = bits(dist[:, None, :] * slopes[None, :, None])
    block, inner = np.arange(SEQ) // P, np.arange(SEQ) % P
    q_rows = np.zeros((CONST_ROWS, HEADS, SEQ))
    k_rows = np.zeros((CONST_ROWS, HEADS, SEQ))
    for r in range(NT):
        q_rows[r] = np.sign(block - r)
        k_rows[r] = slopes[:, None] * (inner * (block == r))
        q_rows[NT + r] = inner * (block == r)
        k_rows[NT + r] = -slopes[:, None] * np.sign(r - block)
        q_rows[2 * NT + r] = -P * np.abs(block - r)
        k_rows[2 * NT + r] = slopes[:, None] * (block == r)
    k_rows[3 * NT:] = 1.0
    pick = np.zeros((P, EXPERTS, P))
    for e in range(EXPERTS):
        for k in range(3):
            pick[k * EXPERTS + e, e, :] = 1.0
    return {"ident": np.eye(P, dtype=np.float32), "identb": bits(np.eye(P)), "diag": diag,
            "q_rows": bits(q_rows), "k_rows": bits(k_rows), "pick": bits(pick)}


def kernel(**inputs):
    import concourse.bacc as bacc
    from concourse.bass_utils import run_bass_kernel_spmd as run

    a = {k: np.asarray(v) for k, v in inputs.items()}
    c = np.ascontiguousarray
    w_heads = a["L0_attn_qkv_w"].reshape(HEADS, 3, DH, D)
    b_heads = a["L0_attn_qkv_b"].reshape(HEADS, 3, DH)
    col = lambda v: c(v.reshape(D, 1))
    arrays = {
        "x": a["L0_attn_x"],
        "wq": c(w_heads[:, 0].reshape(D, D).T), "wk": c(w_heads[:, 1].reshape(D, D).T),
        "wv": c(w_heads[:, 2].reshape(D, D).T), "wo": c(a["L0_attn_out_w"].T),
        "bq": col(b_heads[:, 0]), "bk": col(b_heads[:, 1]), "bv": c(b_heads[:, 2].reshape(D)),
        "bo": a["L0_attn_out_b"],
        "route_w": c(a["L0_ffn_router_w"].T), "route_b": a["L0_ffn_router_b"], "lora_a": a["L0_ffn_lora_A"],
        "lora_b": c(a["L0_ffn_lora_B"].reshape(LORA_E * RANK, D)), "base_w": c(a["L0_ffn_base_w"].T),
        "base_b": a["L0_ffn_base_b"].reshape(1, D),
        "decay": col(a["L1_attn_time_decay"]), "ln_g": col(a["L1_attn_ln_g"]), "ln_b": col(a["L1_attn_ln_b"]),
        "mix_k": col(a["L1_attn_time_mix_k"]), "mix_v": col(a["L1_attn_time_mix_v"]),
        "mix_r": col(a["L1_attn_time_mix_r"]),
        "wkk": c(a["L1_attn_Wk"].T), "wkv": c(a["L1_attn_Wv"].T), "wkr": c(a["L1_attn_Wr"].T),
        "wko": c(a["L1_attn_Wo"].T),
        "w_gate": a["L1_ffn_W_gate"], "w1": a["L1_ffn_W1"], "w2": a["L1_ffn_W2"],
        "b1": c(a["L1_ffn_b1"].reshape(EXPERTS * HB, P).T), "b2": a["L1_ffn_b2"],
    }
    arrays.update(shape_constants())
    nc = bacc.Bacc("TRN2", target_bir_lowering=False, num_devices=1)
    t = {k: nc.dram_tensor(f"in_{k}", v.shape, mybir.dt.from_np(v.dtype), kind="ExternalInput").ap()
         for k, v in arrays.items()}
    t.update({k: t[k].bitcast(BF16) for k in ("identb", "diag", "q_rows", "k_rows", "pick")})
    t["out"] = nc.dram_tensor("out", _OUT, F32, kind="ExternalOutput").ap()
    t["parts"] = nc.dram_tensor("qk_parts_dram", (2, 3, P, SEQ), BF16, kind="Internal").ap()
    layer_norms_attention_lora_wkv_moe_kernel(nc, t)
    r = run(nc, [{f"in_{k}": v for k, v in arrays.items()}], core_ids=[0])
    return r.results[0]["out"]
```
